# Optimizing a Trainium2 kernel written in Bass

```python
import numpy as np
import jax
import jax.numpy as jnp

def _softmax(x, axis=-1):
    return jax.nn.softmax(x, axis=axis)

def _gelu(x):
    return jax.nn.gelu(x, approximate=True)

def _silu(x):
    return jax.nn.silu(x)

def _sigmoid(x):
    return jax.nn.sigmoid(x)

def _layernorm(x, axis=-1, eps=1e-05):
    m = jnp.mean(x, axis=axis, keepdims=True)
    v = jnp.var(x, axis=axis, keepdims=True)
    return (x - m) / jnp.sqrt(v + eps)

def _scatter_add(tgt, idx, src, axis=0):
    return tgt.at[idx].add(src)

def _segment_sum(src, seg, n):
    return jax.ops.segment_sum(src, seg, n)
kernel_name = 'mk_gnn_preln_d1_gnn_r8_7dddfc'

def setup_inputs(seed: int=0):
    np.random.seed(seed)
    _w = jnp.asarray

    def _rec_inputs():
        import jax
        import jax.numpy as jnp
        _gk = jax.random.key(seed)
        x = -0.0003713 + 1 * jax.random.normal(jax.random.fold_in(_gk, 1), (6250, 256), jnp.float32)
        _s = jax.random.randint(jax.random.fold_in(_gk, 2), (50000,), 0, 6250, jnp.int32)
        _d = jax.random.randint(jax.random.fold_in(_gk, 3), (50000,), 0, 6250, jnp.int32)
        _loop = jnp.arange(6250, dtype=jnp.int32)
        src = jnp.concatenate([_s, _d, _loop])
        dst = jnp.concatenate([_d, _s, _loop])
        _o = jnp.argsort(dst, stable=True)
        src = src[_o]
        dst = dst[_o]
        return (x, src, dst)
    x, src, dst = _rec_inputs()

    def _L0_gnn_setup():
        import jax, jax.numpy as jnp
        import numpy as np
        N, E, D, K, L = (6250, 200000, 256, 4, 2)
        TAU = 1.0

        def _scatter_mean(src, row, num_segments):
            sums = jax.ops.segment_sum(src, row, num_segments=num_segments)
            cnt = jax.ops.segment_sum(jnp.ones((src.shape[0],), dtype=src.dtype), row, num_segments=num_segments)
            return sums / jnp.maximum(cnt, 1.0)[:, None]
        key = jax.random.key(seed)
        k1, k2, k3, k4, k5 = jax.random.split(key, 5)
        x = jax.random.normal(k1, (N, D), dtype=jnp.float32)
        edge_index = jax.random.randint(k2, (2, E), 0, N, dtype=jnp.int64)
        lim_w = float(np.sqrt(6.0 / (2 * D + D)))
        W = jax.random.uniform(k3, (L, K, 2 * D, D), minval=-lim_w, maxval=lim_w, dtype=jnp.float32)
        lim_e = float(np.sqrt(1.0 / D))
        envW = jax.random.uniform(k4, (L, D, K), minval=-lim_e, maxval=lim_e, dtype=jnp.float32)
        envb = jax.random.uniform(k5, (L, K), minval=-lim_e, maxval=lim_e, dtype=jnp.float32)
        return {'x': x, 'edge_index': edge_index, 'W': W, 'envW': envW, 'envb': envb}
    _L0_gnn_all = _L0_gnn_setup()
    _L0_gnn_in = {k: v for k, v in _L0_gnn_all.items() if k in ('W', 'envW', 'envb')}
    del _L0_gnn_all
    return {'x': x, 'src': src, 'dst': dst, 'L0_gnn_W': _L0_gnn_in['W'], 'L0_gnn_envW': _L0_gnn_in['envW'], 'L0_gnn_envb': _L0_gnn_in['envb']}

def reference(x, src, dst, L0_gnn_W, L0_gnn_envW, L0_gnn_envb):
    import jax
    import jax.numpy as jnp

    def _L0_gnn_ref(x, edge_index, W, envW, envb):
        import jax, jax.numpy as jnp
        import numpy as np
        N, E, D, K, L = (6250, 200000, 256, 4, 2)
        TAU = 1.0

        def _scatter_mean(src, row, num_segments):
            sums = jax.ops.segment_sum(src, row, num_segments=num_segments)
            cnt = jax.ops.segment_sum(jnp.ones((src.shape[0],), dtype=src.dtype), row, num_segments=num_segments)
            return sums / jnp.maximum(cnt, 1.0)[:, None]
        row, col = (edge_index[0], edge_index[1])
        z = x
        for l in range(L):
            logits = z @ envW[l] + envb[l]
            weights = jax.nn.softmax(logits / TAU, axis=-1)
            agg = _scatter_mean(z[col], row, N)
            combined = jnp.concatenate([agg, z], axis=-1)
            outputs = jnp.einsum('nd,kdo->nko', combined, W[l]) + z[:, None, :]
            z = jnp.einsum('nk,nko->no', weights, outputs)
            z = jax.nn.relu(z)
        return z
    edge_index = jnp.stack([src, dst])
    h = jnp.maximum(_layernorm(x, axis=-1), 0.0)
    x = x + _L0_gnn_ref(h, edge_index, L0_gnn_W, L0_gnn_envW, L0_gnn_envb)
    return x

_drawn_inputs = setup_inputs


def setup_inputs(seed=0):
    import zlib

    import numpy as np

    out = dict(_drawn_inputs(seed))
    spreads = {}
    factors = {'L0_gnn_envb': 4.672}
    for name, (base, spread) in spreads.items():
        noise = np.random.default_rng([zlib.crc32(name.encode()), seed]).standard_normal(out[name].shape)
        drawn = base * np.exp(spread * noise) if base else spread * noise
        out[name] = jnp.asarray(drawn.astype(out[name].dtype))
    for name, factor in factors.items():
        out[name] = (out[name] * factor).astype(out[name].dtype)
    return out
```

```python
from contextlib import ExitStack

import concourse.bass as bass
from concourse import mybir

P = 128
ALU = mybir.AluOpType
ACT = mybir.ActivationFunctionType
AX = mybir.AxisListType
F32 = mybir.dt.float32
I32 = mybir.dt.int32
LN_EPS = 1e-5

RING = 16
ROW = 264
NO_NODE = 1 << 20
LOAD = 7


def gnn_kernel(nc, x, src, dst, W, envW, envb, out):
    N, D = x.shape
    E = src.shape[0]
    L, K, D2, _ = W.shape
    DC = D // P
    CC = D2 // P
    NB = -(-N // P)
    TAIL = N - (NB - 1) * P
    GROUPS = -(-E // (2 * P * RING))
    PAIRS = GROUPS * RING
    CH = next(c for c in range(1, 99) if PAIRS % c == 0 and PAIRS // c <= P)
    PR = PAIRS // CH
    FULL, REST = divmod(E, 2 * P)
    XG = -(-NB // LOAD)
    SLOTS = 2 * RING
    HALF = K * D // 2

    ctx = ExitStack()

    def sb(name, shape, dt=F32):
        return ctx.enter_context(nc.sbuf_tensor(name, shape, dt))

    def psum(name, shape):
        return ctx.enter_context(nc.psum_tensor(name, shape, F32))

    def sem(name):
        return ctx.enter_context(nc.semaphore(name))

    with ctx:
        z_dram = [nc.dram_tensor(f"z{l}_dram", (NB * P, D), F32).ap() for l in range(L)]

        x_sb = sb("x_sb", [P, NB, D])
        w_sb = sb("w_sb", [P, L, CC, K, D])
        envw_sb = sb("envw_sb", [P, L, DC, K])
        envb_sb = sb("envb_sb", [1, L, K])
        ring = sb("ring", [P, RING, 2, ROW])
        ident = sb("ident", [P, P])
        ones_row = sb("ones_row", [1, P])
        ones_col = sb("ones_col", [P, 1])
        node0 = sb("node0", [P, P])
        block_base = sb("block_base", [P, NB])
        block_end = sb("block_end", [P, NB])
        src_t = sb("src_t", [P, (GROUPS + 1) * SLOTS], I32)
        dst_t = sb("dst_t", [P, PAIRS * 2])
        gather_idx = sb("gather_idx", [P, SLOTS], I32)
        plan_f = sb("plan_f", [1, 2 * NB + 2])
        plan = sb("plan", [1, 2 * NB + 2], I32)
        hi_raw = sb("hi_raw", [1, NB + 1])
        unsorted = sb("unsorted", [1, 2])
        nodes = sb("nodes", [P, P])
        onehot = sb("onehot", [P, 2, P])
        z_in = sb("z_in", [P, D])
        zT = sb("zT", [P, DC, P])
        mean = sb("mean", [P, D])
        meanT = sb("meanT", [P, DC, P])
        cnt = sb("cnt", [P, 2])
        negmax = sb("negmax", [P, 1])
        ex = sb("ex", [P, K + 1])
        rsum = sb("rsum", [P, 1])
        wts = sb("wts", [P, K + 1])
        mix = sb("mix", [P, D])
        z_out = sb("z_out", [P, D])

        agg_ps = psum("agg_ps", [P, D + 1])
        zT_ps = psum("zT_ps", [P, DC, P])
        mT_ps = psum("mT_ps", [P, DC, P])
        lg_ps = psum("lg_ps", [P, max(K, NB + 1)])
        mix_ps = [psum(f"mix{i}_ps", [P, HALF]) for i in range(2)]
        lg_hi = lg_ps[0:1, 0:NB + 1]
        turn_ps = [agg_ps[:, 0:P], zT_ps[:, 0, :]]

        s_src = sem("src_loaded")
        s_dst = sem("dst_loaded")
        s_nxt = sem("next_dst_loaded")
        s_w = sem("weights_loaded")
        s_x = [sem(f"x{g}_loaded") for g in range(XG)]
        s_pad = sem("pads_written")
        s_const = sem("constants_ready")
        s_dve0 = sem("vector_prep_step")
        s_pool0 = sem("gpsimd_prep_step")
        s_conv = sem("dst_as_float")
        s_srcf = sem("src_as_float")
        s_turned = sem("edge_tile_turned")
        s_moved = sem("edge_tile_moved")
        s_cmp = sem("pair_compared")
        s_count = sem("plan_counted")
        s_plan = sem("plan_ready")
        s_tables = sem("edge_tables_ready")
        s_stat = sem("x_stats_ready")
        s_aggr = sem("x_mean_var_ready")
        s_std = sem("x_std_ready")
        s_norm = sem("norm_terms_ready")
        s_h = sem("h_computed")
        s_gath = [[sem(f"gathered{l}_{s}") for s in range(SLOTS)] for l in range(L)]
        s_idx = [[sem(f"idx_staged{l}_{h}") for h in range(2)] for l in range(L)]
        s_landed = [sem(f"pairs_landed{l}") for l in range(L)]
        s_free = [sem(f"pairs_free{l}") for l in range(L)]
        s_ohr = [[sem(f"onehot_ready{l}_{h}") for h in range(2)] for l in range(L)]
        s_ohf = [[sem(f"onehot_free{l}_{h}") for h in range(2)] for l in range(L)]
        s_begun = sem("pairs_begun")
        s_staged_all = sem("staging_over")
        s_nodes = sem("nodes_ready")
        s_zin = sem("z_loaded")
        s_cmax = sem("count_clamped")
        s_rcnt = sem("count_inverted")
        s_mean = sem("mean_ready")
        s_zturn = sem("z_turned")
        s_zT = sem("zT_ready")
        s_mturn = sem("mean_turned")
        s_mT = sem("meanT_ready")
        s_logit = sem("logits_ready")
        s_nmax = sem("negmax_ready")
        s_ex = sem("exp_ready")
        s_rsum = sem("sum_inverted")
        s_wts = sem("weights_ready")
        s_zs = sem("z_scaled")
        s_half = [sem(f"mix_half{i}_ready") for i in range(2)]
        s_mix = [sem(f"mix_step{k}") for k in range(K - 1)]
        s_over = sem("block_over")
        s_res = sem("result_ready")
        s_zfree = sem("z_out_free")
        s_stored = sem("z_stored")
        s_hst = [sem(f"h{g}_stored") for g in range(XG)]

        edge_ctx = ExitStack()

        def ed(name, shape, dt=F32):
            return edge_ctx.enter_context(nc.sbuf_tensor(name, shape, dt))

        with edge_ctx:
            src_i = ed("src_i", [PR, CH, 2 * P], I32)
            dst_i = ed("dst_i", [PR, CH, 2 * P], I32)
            nxt_i = ed("nxt_i", [PR, CH, 2 * P], I32)
            src_f = ed("src_f", [PR, CH, 2 * P])
            dst_f = ed("dst_f", [PR, CH, 2 * P])
            nxt_f = ed("nxt_f", [PR, CH, 2 * P])
            compared = ed("compared", [PR, CH, NB])
            falls = ed("falls", [PR, 1])
            stats = ed("stats", [P, NB, 6])
            mv = ed("mv", [P, NB, 2])
            std = ed("std", [P, NB])
            all_pairs = ed("all_pairs", [1, 1])
            rstd = ed("rstd", [P, NB])
            nbias = ed("nbias", [P, NB])
            h_sb = ed("h_sb", [P, 2, LOAD, D])
            eps = ed("eps", [P, 1])

            def load_edges(eng, tile_i, array, first, signal):
                n = E - first
                full, rest = divmod(n, 2 * P)
                whole = min(full // PR, CH)
                eng.dma_start(tile_i[:, 0:whole, :], array[first:first + whole * PR * 2 * P].rearrange(
                    "(c p e) -> p c e", p=PR, e=2 * P)).then_inc(signal, 16)
                left = full - whole * PR
                if left:
                    a = first + whole * PR * 2 * P
                    eng.dma_start(tile_i[0:left, whole, :], array[a:a + left * 2 * P].rearrange(
                        "(p e) -> p e", e=2 * P)).then_inc(signal, 16)
                a = first + full * 2 * P
                eng.dma_start(tile_i[left:left + 1, whole, 0:rest], array[a:a + rest].rearrange(
                    "(o e) -> o e", o=1)).then_inc(signal, 16)
                return 16 * (3 if left else 2)

            WHOLE = FULL // PR
            EDGE_DMAS = 16 * (3 if FULL - WHOLE * PR else 2)
            NTURN = CH * 2
            LASTX = (XG - 1) * LOAD

            def xrange(g):
                return g * LOAD, min((g + 1) * LOAD, NB)

            with nc.Block() as block:

                @block.sync
                def _(sp):
                    sp.wait_ge(s_pad, 3)
                    load_edges(sp, dst_i, dst, 0, s_dst)
                    load_edges(sp, nxt_i, dst, 1, s_nxt)
                    load_edges(sp, src_i, src, 0, s_src)
                    for g in range(XG):
                        a, b = xrange(g)
                        full = b - 1 if b == NB and TAIL < P else b
                        if b == NB and TAIL < P:
                            sp.wait_ge(s_pad, 4)
                            sp.dma_start(x_sb[0:TAIL, NB - 1, :], x[(NB - 1) * P:N, :]).then_inc(s_x[g], 16)
                        if full > a:
                            sp.dma_start(x_sb[:, a:full, :], x[a * P:full * P, :].rearrange(
                                "(t p) d -> p t d", p=P)).then_inc(s_x[g], 16)
                    for l in range(L):
                        for c in range(CC):
                            sp.dma_start(w_sb[:, l, c, :, :], W[l, :, c * P:(c + 1) * P, :].rearrange(
                                "k p o -> p k o")).then_inc(s_w, 16)
                        with nc.allow_non_contiguous_dma(reason="16-byte rows, once"):
                            sp.dma_start(envw_sb[:, l, :, :], envW[l].rearrange(
                                "(c p) k -> p c k", p=P)).then_inc(s_w, 16)
                    sp.dma_start(envb_sb[0:1, :, :], envb.rearrange("(o l) k -> o l k", o=1)).then_inc(s_w, 16)
                    for g in range(XG):
                        a, b = xrange(g)
                        sp.wait_ge(s_h, b)
                        sp.dma_start(z_dram[0][a * P:b * P, :].rearrange("(t p) d -> p t d", p=P),
                                     h_sb[:, g % 2, 0:b - a, :]).then_inc(s_hst[g], 16)
                    sp.wait_ge(s_w, 16 * (L * (CC + 1) + 1))
                    for g in range(XG):
                        sp.wait_ge(s_hst[g], 16)

                @block.gpsimd
                def _(pool):
                    last = CH - 1
                    nc.gpsimd.memset(dst_i[:, last, :], NO_NODE).then_inc(s_pad, 1)
                    nc.gpsimd.memset(nxt_i[:, last, :], NO_NODE).then_inc(s_pad, 1)
                    nc.gpsimd.memset(src_i[:, last, :], 0).then_inc(s_pad, 1)
                    nc.gpsimd.memset(x_sb[:, NB - 1, :], 0.0).then_inc(s_pad, 1)
                    nc.gpsimd.memset(ident[:], 0.0).then_inc(s_pool0, 1)
                    pool.wait_ge(s_pool0, 1)
                    nc.gpsimd.affine_select(out=ident[:], in_=ident[:], compare_op=ALU.not_equal, fill=1.0, base=0,
                                            pattern=[[-1, P]], channel_multiplier=1).then_inc(s_const, 1)
                    nc.gpsimd.iota(node0[:], pattern=[[1, P]], base=0, channel_multiplier=0,
                                   allow_small_or_imprecise_dtypes=True).then_inc(s_const, 1)
                    nc.gpsimd.iota(block_base[:], pattern=[[P, NB]], base=0, channel_multiplier=0,
                                   allow_small_or_imprecise_dtypes=True).then_inc(s_const, 1)
                    nc.gpsimd.iota(block_end[:], pattern=[[P, NB]], base=P, channel_multiplier=0,
                                   allow_small_or_imprecise_dtypes=True).then_inc(s_const, 1)
                    nc.gpsimd.memset(ones_row[:], 1.0).then_inc(s_const, 1)
                    nc.gpsimd.memset(ones_col[:], 1.0).then_inc(s_const, 1)
                    nc.gpsimd.memset(ring[:, :, :, D:D + 1], 1.0).then_inc(s_const, 1)
                    nc.gpsimd.memset(src_t[:, GROUPS * SLOTS:], 0).then_inc(s_const, 1)
                    nc.gpsimd.memset(eps[:], LN_EPS).then_inc(s_const, 1)
                    pool.wait_ge(s_src, EDGE_DMAS)
                    nc.gpsimd.tensor_copy(src_f[:], src_i[:]).then_inc(s_srcf, 1)

                @block.vector
                def _(dve):
                    dve.wait_ge(s_dst, EDGE_DMAS)
                    nc.vector.tensor_copy(dst_f[:], dst_i[:]).then_inc(s_conv, 1)
                    dve.wait_ge(s_nxt, EDGE_DMAS)
                    nc.vector.tensor_copy(nxt_f[:], nxt_i[:]).then_inc(s_dve0, 1)
                    dve.wait_ge(s_dve0, 1)
                    dve.wait_ge(s_conv, 1)
                    nc.vector.tensor_tensor(nxt_f[:], dst_f[:], nxt_f[:], ALU.is_gt).then_inc(s_dve0, 1)
                    dve.wait_ge(s_dve0, 2)
                    nc.vector.reduce_sum(falls[:], nxt_f[:], AX.XY).then_inc(s_cmp, 1)
                    dve.wait_ge(s_const, 9)
                    for c in range(CH):
                        nc.vector.tensor_scalar(compared[:, c, :], block_end[0:PR, :], dst_f[:, c, 0:1], None,
                                                ALU.is_gt).then_inc(s_cmp, 1)
                    dve.wait_ge(s_count, 1)
                    nc.vector.tensor_copy(hi_raw[:], lg_hi).then_inc(s_dve0, 1)
                    dve.wait_ge(s_dve0, 3)
                    nc.vector.tensor_scalar(unsorted[:, 0:1], hi_raw[:, NB:NB + 1], 1.0, None,
                                            ALU.min).then_inc(s_dve0, 1)
                    nc.vector.tensor_scalar(hi_raw[:, 0:NB], hi_raw[:, 0:NB], 1.0, None, ALU.max).then_inc(s_dve0, 1)
                    dve.wait_ge(s_dve0, 5)
                    nc.vector.tensor_scalar(unsorted[:, 1:2], unsorted[:, 0:1], -1.0, 1.0, ALU.mult,
                                            ALU.add).then_inc(s_dve0, 1)
                    dve.wait_ge(s_dve0, 6)
                    lohi = plan_f[:, 0:2 * NB].rearrange("o (b two) -> o b two", two=2)
                    nc.vector.memset(lohi[:, 0, 0:1], 0.0).then_inc(s_dve0, 1)
                    nc.vector.tensor_scalar(lohi[:, 1:NB, 0], hi_raw[:, 0:NB - 1], -1.0, unsorted[:, 1:2],
                                            ALU.add, ALU.mult).then_inc(s_dve0, 1)
                    nc.vector.tensor_scalar(all_pairs[:], unsorted[:, 0:1], float(PAIRS), None,
                                            ALU.mult).then_inc(s_dve0, 1)
                    dve.wait_ge(s_dve0, 9)
                    nc.vector.tensor_scalar(lohi[:, :, 1], hi_raw[:, 0:NB], all_pairs[:], None,
                                            ALU.max).then_inc(s_dve0, 1)
                    nc.vector.tensor_scalar(plan_f[:, 2 * NB:], unsorted[:], float(NB - 1), 1.0, ALU.mult,
                                            ALU.add).then_inc(s_dve0, 1)
                    dve.wait_ge(s_dve0, 11)
                    nc.vector.tensor_copy(plan[:], plan_f[:]).then_inc(s_plan, 1)
                    dst_v = dst_t[:].rearrange("p (v h) -> p v h", h=2)
                    src_v = src_t[:, 0:PAIRS * 2].rearrange("p (v h) -> p v h", h=2)
                    for i in range(2 * NTURN):
                        c, h = (i % NTURN) // 2, i % 2
                        to = (dst_v if i < NTURN else src_v)[:, c * PR:(c + 1) * PR, h]
                        dve.wait_ge(s_turned, i + 1)
                        nc.vector.tensor_copy(to, turn_ps[i % 2][:, 0:PR]).then_inc(s_moved, 1)
                    for g in range(XG):
                        a, b = xrange(g)
                        both = b == NB and TAIL < P and b - 1 > a
                        dve.wait_ge(s_x[g], 32 if both else 16)
                        for t in range(a, b):
                            nc.vector.bn_stats(stats[:, t, :], x_sb[:, t, :]).then_inc(s_stat, 1)
                        for t in range(a, b):
                            dve.wait_ge(s_stat, t + 1)
                            nc.vector.bn_aggr(mv[:, t, :], stats[:, t, :]).then_inc(s_aggr, 1)
                        dve.wait_ge(s_std, g + 1)
                        nc.vector.reciprocal(rstd[:, a:b], std[:, a:b]).then_inc(s_norm, 1)
                        dve.wait_ge(s_norm, 2 * g + 1)
                        nc.vector.scalar_tensor_tensor(out=nbias[:, a:b], in0=mv[:, a:b, 0], scalar=-1.0,
                                                       in1=rstd[:, a:b], op0=ALU.mult,
                                                       op1=ALU.mult).then_inc(s_norm, 1)

                @block.scalar
                def _(act):
                    act.wait_ge(s_const, 9)
                    for g in range(XG):
                        a, b = xrange(g)
                        act.wait_ge(s_aggr, b)
                        nc.scalar.activation(std[:, a:b], mv[:, a:b, 1], ACT.Sqrt, bias=eps[:, 0:1]).then_inc(s_std, 1)
                        act.wait_ge(s_norm, 2 * g + 2)
                        if g >= 2:
                            act.wait_ge(s_hst[g - 2], 16)
                        for t in range(a, b):
                            nc.scalar.activation(h_sb[:, g % 2, t - a, :], x_sb[:, t, :], ACT.Relu,
                                                 bias=nbias[:, t:t + 1], scale=rstd[:, t:t + 1]).then_inc(s_h, 1)

                @block.tensor
                def _(pe):
                    pe.wait_ge(s_const, 9)
                    pe.wait_ge(s_cmp, 1 + CH)
                    for c in range(CH):
                        pe.matmul(lg_hi[:, 0:NB], ones_col[0:PR, :], compared[:, c, :], start=(c == 0),
                                  stop=(c == CH - 1))
                    pe.matmul(lg_hi[:, NB:NB + 1], ones_col[0:PR, :], falls[:], start=True,
                              stop=True).then_inc(s_count, 1)
                    for i in range(2 * NTURN):
                        c, h = (i % NTURN) // 2, i % 2
                        if i == NTURN:
                            pe.wait_ge(s_srcf, 1)
                        rows = (dst_f if i < NTURN else src_f)[:, c, h * P:(h + 1) * P]
                        if i >= 2:
                            pe.wait_ge(s_moved, i - 1)
                        pe.transpose(turn_ps[i % 2][:, 0:PR], rows, ident[0:PR, 0:PR]).then_inc(s_turned, 1)

            def block_no(eng, p, b):
                return nc.s_assert_within(eng.snap(p + b), 0, NB - 1,
                                          skip_runtime_bounds_check_because="passes * blocks_per_pass = NB")

            def passes_of(eng):
                return (eng.value_load(plan[0:1, 2 * NB:2 * NB + 1], min_val=1, max_val=NB),
                        eng.value_load(plan[0:1, 2 * NB + 1:2 * NB + 2], min_val=1, max_val=NB))

            def pairs_of(eng, blk):
                lo = eng.value_load(plan[0:1, bass.ds(blk * 2, 1)], min_val=0, max_val=PAIRS - 1)
                hi = eng.value_load(plan[0:1, bass.ds(blk * 2 + 1, 1)], min_val=1, max_val=PAIRS)
                return lo, hi

            with nc.Block() as block:

                @block.gpsimd
                def _(pool):
                    passes, _ = passes_of(pool)
                    for l in range(L):
                        if l:
                            pool.wait_ge(s_stored, 16 * NB * l)
                        else:
                            for g in range(XG):
                                pool.wait_ge(s_hst[g], 16)
                        with pool.Fori(0, passes) as p:
                            with pool.Fori(0, GROUPS) as g:
                                turn = pool.snap(p * GROUPS + g)
                                for s in range(SLOTS):
                                    if s % RING == 0:
                                        pool.wait_ge(s_idx[l][s // RING], turn * 16 + 16)
                                    if s % 2 == 0:
                                        pool.wait_ge(s_free[l], turn * RING + (s // 2 + 1))
                                        pool.sem_inc(s_begun, 1)
                                    pool.indirect_dma_start(
                                        out=ring[:, s // 2, s % 2, 0:D], out_offset=None, in_=z_dram[l],
                                        in_offset=bass.IndirectOffsetOnAxis(ap=gather_idx[:, s:s + 1], axis=0),
                                    ).then_inc(s_gath[l][s], 16)

                @block.sync
                def _(sp):
                    passes, _ = passes_of(sp)
                    for l in range(L):
                        if l:
                            for h in range(2):
                                sp.wait_ge(s_idx[l - 1][h], passes * (16 * GROUPS) + 16)
                        for h in range(2):
                            a = h * RING
                            sp.dma_start(gather_idx[:, a:a + RING], src_t[:, a:a + RING]).then_inc(s_idx[l][h], 16)
                        with sp.Fori(0, passes) as p:
                            with sp.Fori(0, GROUPS) as g:
                                turn = sp.snap(p * GROUPS + g)
                                for s in range(SLOTS):
                                    sp.wait_ge(s_gath[l][s], turn * 16 + 16)
                                    if s % 2 == 1:
                                        sp.sem_inc(s_landed[l], 1)
                                    if s % RING == RING - 1:
                                        a = s + 1 - RING
                                        sp.dma_start(gather_idx[:, a:a + RING],
                                                     src_t[:, bass.ds(g * SLOTS + (SLOTS + a), RING)]).then_inc(
                                                         s_idx[l][a // RING], 16)
                    for h in range(2):
                        sp.wait_ge(s_idx[L - 1][h], passes * (16 * GROUPS) + 16)
                    sp.sem_inc(s_staged_all, 1)

                @block.vector
                def _(dve):
                    passes, blocks = passes_of(dve)
                    dve.sem_inc(s_over, 1)
                    dve.sem_inc(s_mean, 1)
                    for l in range(L):
                        base = l * NB
                        with dve.Fori(0, passes) as p:
                            with dve.Fori(0, blocks) as b:
                                blk = block_no(dve, p, b)
                                done = dve.snap(blk + base)
                                now = dve.snap(done + 1)
                                lo, hi = pairs_of(dve, blk)
                                step0 = dve.snap(p * PAIRS + b)
                                nc.vector.tensor_scalar(nodes[:], node0[:], block_base[:, bass.ds(blk, 1)], None,
                                                        ALU.add).then_inc(s_nodes, 1)
                                with dve.Fori(lo, hi) as u:
                                    dve.wait_ge(s_nodes, now)
                                    step = dve.snap(step0 + u)
                                    for h in range(2):
                                        dve.wait_ge(s_ohf[l][h], step + 1)
                                        nc.vector.tensor_scalar(onehot[:, h, :], nodes[:],
                                                                dst_t[:, bass.ds(u * 2 + h, 1)], None,
                                                                ALU.is_equal).then_inc(s_ohr[l][h], 1)
                                dve.wait_ge(s_ohf[l][1], step0 + hi + 1)
                                nc.vector.tensor_scalar(cnt[:, 0:1], agg_ps[:, D:D + 1], 1.0, None,
                                                        ALU.max).then_inc(s_cmax, 1)
                                dve.wait_ge(s_cmax, now)
                                nc.vector.reciprocal(cnt[:, 1:2], cnt[:, 0:1]).then_inc(s_rcnt, 1)
                                dve.wait_ge(s_rcnt, now)
                                nc.vector.tensor_scalar(mean[:], agg_ps[:, 0:D], cnt[:, 1:2], None,
                                                        ALU.mult).then_inc(s_mean, 1)
                                dve.wait_ge(s_logit, now)
                                nc.vector.tensor_reduce(negmax[:], lg_ps[:, 0:K], AX.X, ALU.max,
                                                        negate=True).then_inc(s_nmax, 1)
                                dve.wait_ge(s_mturn, now)
                                nc.vector.tensor_copy(meanT[:], mT_ps[:]).then_inc(s_mT, 1)
                                dve.wait_ge(s_ex, now)
                                nc.vector.reciprocal(rsum[:], ex[:, K:K + 1]).then_inc(s_rsum, 1)
                                dve.wait_ge(s_rsum, now)
                                nc.vector.tensor_scalar(wts[:], ex[:], rsum[:, 0:1], None, ALU.mult).then_inc(s_wts, 1)
                                dve.wait_ge(s_wts, now)
                                dve.wait_ge(s_zs, now)
                                for k in range(K):
                                    i, j = divmod(k * D, HALF)
                                    if j == 0:
                                        dve.wait_ge(s_half[i], now)
                                    if k:
                                        dve.wait_ge(s_mix[k - 1], now)
                                    nc.vector.scalar_tensor_tensor(out=mix[:], in0=mix_ps[i][:, j:j + D],
                                                                   scalar=wts[:, k:k + 1], in1=mix[:], op0=ALU.mult,
                                                                   op1=ALU.add).then_inc(s_mix[k] if k < K - 1 else s_over, 1)
                                if l == L - 1:
                                    dve.wait_ge(s_over, now + 1)
                                    nc.vector.scalar_tensor_tensor(out=z_out[:], in0=mix[:], scalar=0.0,
                                                                   in1=x_sb[:, bass.ds(blk, 1), :], op0=ALU.max,
                                                                   op1=ALU.add).then_inc(s_res, 1)

                @block.scalar
                def _(act):
                    passes, blocks = passes_of(act)
                    for l in range(L):
                        base = l * NB
                        if l:
                            act.wait_ge(s_stored, 16 * base)
                        with act.Fori(0, passes) as p:
                            with act.Fori(0, blocks) as b:
                                blk = block_no(act, p, b)
                                done = act.snap(blk + base)
                                now = act.snap(done + 1)
                                act.wait_ge(s_over, now)
                                act.dma_start(z_in[:], z_dram[l][bass.ds(blk * P, P), :]).then_inc(s_zin, 16)
                                act.wait_ge(s_zturn, now)
                                nc.scalar.activation(zT[:], zT_ps[:], ACT.Copy).then_inc(s_zT, 1)
                                act.wait_ge(s_nmax, now)
                                nc.scalar.activation(ex[:, 0:K], lg_ps[:, 0:K], ACT.Exp, bias=negmax[:, 0:1],
                                                     accum_out=ex[:, K:K + 1]).then_inc(s_ex, 1)
                                act.wait_ge(s_wts, now)
                                if l == L - 1:
                                    act.wait_ge(s_res, done)
                                nc.scalar.activation(mix[:], z_in[:], ACT.Copy, scale=wts[:, K:K + 1]).then_inc(s_zs, 1)
                                if l < L - 1:
                                    act.wait_ge(s_over, now + 1)
                                    nc.scalar.activation(z_out[:], mix[:], ACT.Relu).then_inc(s_res, 1)
                                    act.wait_ge(s_res, now)
                                    act.dma_start(z_dram[l + 1][bass.ds(blk * P, P), :], z_out[:]).then_inc(s_stored, 16)
                                else:
                                    with act.If(blk < NB - 1):
                                        whole = nc.s_assert_within(blk, 0, NB - 2,
                                                                   skip_runtime_bounds_check_because="just compared")
                                        act.wait_ge(s_res, now)
                                        act.dma_start(out[bass.ds(whole * P, P), :], z_out[:]).then_inc(s_stored, 16)
                                    with act.Else():
                                        act.wait_ge(s_res, now)
                                        act.dma_start(out[(NB - 1) * P:N, :], z_out[0:TAIL, :]).then_inc(s_stored, 16)
                                act.wait_ge(s_stored, now * 16)
                                act.sem_inc(s_zfree, 1)
                    act.wait_ge(s_stored, 16 * L * NB)

                @block.tensor
                def _(pe):
                    passes, blocks = passes_of(pe)
                    for l in range(L):
                        base = l * NB
                        pe.sem_inc(s_free[l], RING)
                        for h in range(2):
                            pe.sem_inc(s_ohf[l][h], 1)

                        def add_tile(u, step, landed, h, first):
                            if h == 0:
                                pe.wait_ge(s_landed[l], landed)
                            pe.wait_ge(s_ohr[l][h], step + 1)
                            return pe.matmul(agg_ps[:, :], onehot[:, h, :],
                                             ring[:, bass.ds(u % RING, 1), h, 0:D + 1], start=first, stop=True,
                                             skip_group_check=True)

                        with pe.Fori(0, passes) as p:
                            with pe.Fori(0, blocks) as b:
                                blk = block_no(pe, p, b)
                                done = pe.snap(blk + base)
                                now = pe.snap(done + 1)
                                lo, hi = pairs_of(pe, blk)
                                step0 = pe.snap(p * PAIRS + b)
                                land0 = pe.snap(p * PAIRS + 1)
                                pe.wait_ge(s_mean, now)
                                for h in range(2):
                                    add_tile(lo, step0 + lo, land0 + lo, h, h == 0).then_inc(s_ohf[l][h], 1)
                                with pe.If(lo + 1 < hi):
                                    with pe.Fori(lo + 1, hi) as u:
                                        add_tile(u, step0 + u, land0 + u, 0, False).then_inc(s_ohf[l][0], 1)
                                        add_tile(u, step0 + u, land0 + u, 1, False).then_inc(s_ohf[l][1], 1)
                                        pe.sem_inc(s_free[l], 1)
                                pe.wait_ge(s_zin, now * 16)
                                for c in range(DC):
                                    last = pe.transpose(zT_ps[:, c, :], z_in[:, c * P:(c + 1) * P], ident[:])
                                last.then_inc(s_zturn, 1)
                                pe.wait_ge(s_zT, now)
                                pe.wait_ge(s_over, now)
                                for c in range(DC):
                                    pe.matmul(lg_ps[:, 0:K], zT[:, c, :], envw_sb[:, l, c, :], start=(c == 0),
                                              stop=False)
                                pe.matmul(lg_ps[:, 0:K], ones_row[:], envb_sb[:, l, :], start=False,
                                          stop=True).then_inc(s_logit, 1)

                                def product(lhsT, c, i, **flags):
                                    w = w_sb[:, l, c, :, :].rearrange("p k o -> p (k o)")
                                    return pe.matmul(mix_ps[i][:, :], lhsT, w[:, i * HALF:(i + 1) * HALF], **flags)

                                for i in range(2):
                                    product(zT[:, 0, :], DC, i, start=True, stop=False)
                                pe.wait_ge(s_mean, now + 1)
                                for c in range(DC):
                                    last = pe.transpose(mT_ps[:, c, :], mean[:, c * P:(c + 1) * P], ident[:])
                                last.then_inc(s_mturn, 1)
                                for i in range(2):
                                    for c in range(1, DC):
                                        product(zT[:, c, :], DC + c, i, start=False, stop=False)
                                pe.wait_ge(s_mT, now)
                                for i in range(2):
                                    for c in range(DC):
                                        last = product(meanT[:, c, :], c, i, start=False, stop=(c == DC - 1))
                                    last.then_inc(s_half[i], 1)
                            pe.drain().then_inc(s_free[l], 1)


_INS = ["x", "src", "dst", "L0_gnn_W", "L0_gnn_envW", "L0_gnn_envb"]


def kernel(**inputs):
    import numpy as np
    import concourse.bacc as bacc
    from concourse.bass_utils import run_bass_kernel_spmd

    nc = bacc.Bacc("TRN2", target_bir_lowering=False, num_devices=1)
    arrays, args = {}, []
    for name in _INS:
        a = np.ascontiguousarray(inputs[name])
        arrays[f"in_{name}"] = a
        args.append(nc.dram_tensor(f"in_{name}", a.shape, mybir.dt.from_np(a.dtype), kind="ExternalInput").ap())
    out = nc.dram_tensor("out_x", arrays["in_x"].shape, F32, kind="ExternalOutput").ap()
    gnn_kernel(nc, *args, out)
    r = run_bass_kernel_spmd(nc, [arrays], core_ids=[0])
    return r.results[0]["out_x"]
```

```python
from contextlib import ExitStack

import concourse.bass as bass
from concourse import mybir

P = 128
ALU = mybir.AluOpType
ACT = mybir.ActivationFunctionType
AX = mybir.AxisListType
F32 = mybir.dt.float32
I32 = mybir.dt.int32
LN_EPS = 1e-5

RING = 16
ROW = 264
NO_NODE = 1 << 20
TURN = 4
PLACES = 2 + (TURN - 1) + TURN
LOAD = 7


def gnn_kernel(nc, x, src, dst, W, envW, envb, out):
    N, D = x.shape
    E = src.shape[0]
    L, K, D2, _ = W.shape
    DC = D // P
    CC = D2 // P
    NB = -(-N // P)
    TAIL = N - (NB - 1) * P
    GROUPS = -(-E // (2 * P * RING))
    PAIRS = GROUPS * RING
    CH = next(c for c in range(1, 99) if PAIRS % c == 0 and PAIRS // c <= P)
    PR = PAIRS // CH
    FULL, REST = divmod(E, 2 * P)
    XG = -(-NB // LOAD)
    SLOTS = 2 * RING
    HALF = K * D // 2

    ctx = ExitStack()

    def sb(name, shape, dt=F32):
        return ctx.enter_context(nc.sbuf_tensor(name, shape, dt))

    def psum(name, shape):
        return ctx.enter_context(nc.psum_tensor(name, shape, F32))

    def sem(name):
        return ctx.enter_context(nc.semaphore(name))

    with ctx:
        z_dram = [nc.dram_tensor(f"z{l}_dram", (NB * P, D), F32).ap() for l in range(L)]

        z_res = sb("z_res", [P, NB + 1, D])
        x_in = sb("x_in", [P, D])
        w_sb = sb("w_sb", [P, L, CC, K, D])
        envw_sb = sb("envw_sb", [P, L, DC, K])
        envb_sb = sb("envb_sb", [1, L, K])
        ring = sb("ring", [P, RING, 2, ROW])
        ident = sb("ident", [P, P])
        ones_row = sb("ones_row", [1, P])
        ones_col = sb("ones_col", [P, 1])
        node0 = sb("node0", [P, P])
        block_base = sb("block_base", [P, NB + 1])
        block_end = sb("block_end", [P, NB])
        src_t = sb("src_t", [P, (GROUPS + 1) * SLOTS], I32)
        dst_t = sb("dst_t", [P, PAIRS * 2])
        gather_idx = sb("gather_idx", [P, SLOTS], I32)
        plan_f = sb("plan_f", [1, 2 * NB + 4])
        plan = sb("plan", [1, 2 * NB + 4], I32)
        hi_raw = sb("hi_raw", [1, NB + 1])
        unsorted = sb("unsorted", [1, 2])
        nodes = sb("nodes", [P, P])
        onehot = sb("onehot", [P, PLACES, 2, P])
        z_in = sb("z_in", [P, D])
        zT = sb("zT", [P, DC, P])
        mean = sb("mean", [P, D])
        meanT = sb("meanT", [P, DC, P])
        cnt = sb("cnt", [P, 2])
        bias = sb("bias", [P, L * K])
        logits = sb("logits", [P, K])
        negmax = sb("negmax", [P, 1])
        ex = sb("ex", [P, K + 1])
        rsum = sb("rsum", [P, 1])
        wts = sb("wts", [P, K + 1])
        mix = sb("mix", [P, D])
        z_out = sb("z_out", [P, D])

        agg_ps = psum("agg_ps", [P, D + 1])
        zT_ps = psum("zT_ps", [P, DC, P])
        mT_ps = psum("mT_ps", [P, DC, P])
        lg_ps = psum("lg_ps", [P, max(K, NB + 1)])
        mix_ps = [psum(f"mix{i}_ps", [P, HALF]) for i in range(2)]
        lg_hi = lg_ps[0:1, 0:NB + 1]
        turn_ps = [agg_ps[:, 0:P], zT_ps[:, 0, :]]

        s_src = sem("src_loaded")
        s_dst = sem("dst_loaded")
        s_nxt = sem("next_dst_loaded")
        s_w = sem("weights_loaded")
        s_x = [sem(f"x{g}_loaded") for g in range(XG)]
        s_pad = sem("pads_written")
        s_const = sem("constants_ready")
        s_dve0 = sem("vector_prep_step")
        s_pool0 = sem("gpsimd_prep_step")
        s_conv = sem("dst_as_float")
        s_srcf = sem("src_as_float")
        s_turned = sem("edge_tile_turned")
        s_moved = sem("edge_tile_moved")
        s_cmp = sem("pair_compared")
        s_count = sem("plan_counted")
        s_plan = sem("plan_ready")
        s_tables = sem("edge_tables_ready")
        s_stat = sem("x_stats_ready")
        s_aggr = sem("x_mean_var_ready")
        s_std = sem("x_std_ready")
        s_norm = sem("norm_terms_ready")
        s_h = sem("h_computed")
        s_gath = [[sem(f"gathered{l}_{s}") for s in range(SLOTS)] for l in range(L)]
        s_idx = [[sem(f"idx_staged{l}_{h}") for h in range(2)] for l in range(L)]
        s_landed = [sem(f"pairs_landed{l}") for l in range(L)]
        s_free = [sem(f"pairs_free{l}") for l in range(L)]
        s_ohr = [sem(f"onehots_ready{l}") for l in range(L)]
        s_ohf = [sem(f"onehots_free{l}") for l in range(L)]
        s_past = sem("act_past_wait")
        s_begun = sem("pairs_begun")
        s_staged_all = sem("staging_over")
        s_nodes = sem("nodes_ready")
        s_zin = sem("z_loaded")
        s_cmax = sem("count_clamped")
        s_rcnt = sem("count_inverted")
        s_mean = sem("mean_ready")
        s_zturn = sem("z_turned")
        s_zT = sem("zT_ready")
        s_mturn = sem("mean_turned")
        s_mT = sem("meanT_ready")
        s_bias = sem("biases_spread")
        s_logit = sem("logits_ready")
        s_biased = sem("logits_biased")
        s_nmax = sem("negmax_ready")
        s_ex = sem("exp_ready")
        s_rsum = sem("sum_inverted")
        s_wts = sem("weights_ready")
        s_zs = sem("z_scaled")
        s_half = [sem(f"mix_half{i}_ready") for i in range(2)]
        s_mix = [sem(f"mix_step{k}") for k in range(K - 1)]
        s_over = sem("block_over")
        s_res = sem("result_ready")
        s_stored = [sem(f"z{l + 1}_stored") for l in range(L - 1)]
        s_xio = sem("x_loaded_or_out_stored")
        s_hst = [sem(f"h{g}_stored") for g in range(XG)]

        edge_ctx = ExitStack()

        def ed(name, shape, dt=F32):
            return edge_ctx.enter_context(nc.sbuf_tensor(name, shape, dt))

        with edge_ctx:
            src_i = ed("src_i", [PR, CH, 2 * P], I32)
            dst_i = ed("dst_i", [PR, CH, 2 * P], I32)
            nxt_i = ed("nxt_i", [PR, CH, 2 * P], I32)
            src_f = ed("src_f", [PR, CH, 2 * P])
            dst_f = ed("dst_f", [PR, CH, 2 * P])
            nxt_f = ed("nxt_f", [PR, CH, 2 * P])
            compared = ed("compared", [PR, CH, NB])
            falls = ed("falls", [PR, 1])
            stats = ed("stats", [P, NB, 6])
            mv = ed("mv", [P, NB, 2])
            std = ed("std", [P, NB])
            all_pairs = ed("all_pairs", [1, 1])
            rstd = ed("rstd", [P, NB])
            nbias = ed("nbias", [P, NB])
            eps = ed("eps", [P, 1])

            def load_edges(eng, tile_i, array, first, signal):
                n = E - first
                full, rest = divmod(n, 2 * P)
                whole = min(full // PR, CH)
                eng.dma_start(tile_i[:, 0:whole, :], array[first:first + whole * PR * 2 * P].rearrange(
                    "(c p e) -> p c e", p=PR, e=2 * P)).then_inc(signal, 16)
                left = full - whole * PR
                if left:
                    a = first + whole * PR * 2 * P
                    eng.dma_start(tile_i[0:left, whole, :], array[a:a + left * 2 * P].rearrange(
                        "(p e) -> p e", e=2 * P)).then_inc(signal, 16)
                a = first + full * 2 * P
                eng.dma_start(tile_i[left:left + 1, whole, 0:rest], array[a:a + rest].rearrange(
                    "(o e) -> o e", o=1)).then_inc(signal, 16)
                return 16 * (3 if left else 2)

            WHOLE = FULL // PR
            EDGE_DMAS = 16 * (3 if FULL - WHOLE * PR else 2)
            NTURN = CH * 2
            LASTX = (XG - 1) * LOAD

            def xrange(g):
                return g * LOAD, min((g + 1) * LOAD, NB)

            with nc.Block() as block:

                @block.sync
                def _(sp):
                    sp.wait_ge(s_pad, 3)
                    load_edges(sp, dst_i, dst, 0, s_dst)
                    load_edges(sp, nxt_i, dst, 1, s_nxt)
                    load_edges(sp, src_i, src, 0, s_src)
                    for g in range(XG):
                        a, b = xrange(g)
                        full = b - 1 if b == NB and TAIL < P else b
                        if b == NB and TAIL < P:
                            sp.wait_ge(s_pad, 4)
                            sp.dma_start(z_res[0:TAIL, NB - 1, :], x[(NB - 1) * P:N, :]).then_inc(s_x[g], 16)
                        if full > a:
                            sp.dma_start(z_res[:, a:full, :], x[a * P:full * P, :].rearrange(
                                "(t p) d -> p t d", p=P)).then_inc(s_x[g], 16)
                    for l in range(L):
                        for c in range(CC):
                            sp.dma_start(w_sb[:, l, c, :, :], W[l, :, c * P:(c + 1) * P, :].rearrange(
                                "k p o -> p k o")).then_inc(s_w, 16)
                        with nc.allow_non_contiguous_dma(reason="16-byte rows, once"):
                            sp.dma_start(envw_sb[:, l, :, :], envW[l].rearrange(
                                "(c p) k -> p c k", p=P)).then_inc(s_w, 16)
                    sp.dma_start(envb_sb[0:1, :, :], envb.rearrange("(o l) k -> o l k", o=1)).then_inc(s_w, 16)
                    for g in range(XG):
                        a, b = xrange(g)
                        sp.wait_ge(s_h, b)
                        sp.dma_start(z_dram[0][a * P:b * P, :].rearrange("(t p) d -> p t d", p=P),
                                     z_res[:, a:b, :]).then_inc(s_hst[g], 16)
                    sp.wait_ge(s_w, 16 * (L * (CC + 1) + 1))
                    for g in range(XG):
                        sp.wait_ge(s_hst[g], 16)

                @block.gpsimd
                def _(pool):
                    last = CH - 1
                    nc.gpsimd.memset(dst_i[:, last, :], NO_NODE).then_inc(s_pad, 1)
                    nc.gpsimd.memset(nxt_i[:, last, :], NO_NODE).then_inc(s_pad, 1)
                    nc.gpsimd.memset(src_i[:, last, :], 0).then_inc(s_pad, 1)
                    nc.gpsimd.memset(z_res[:, NB - 1:NB + 1, :], 0.0).then_inc(s_pad, 1)
                    nc.gpsimd.memset(ident[:], 0.0).then_inc(s_pool0, 1)
                    pool.wait_ge(s_pool0, 1)
                    nc.gpsimd.affine_select(out=ident[:], in_=ident[:], compare_op=ALU.not_equal, fill=1.0, base=0,
                                            pattern=[[-1, P]], channel_multiplier=1).then_inc(s_const, 1)
                    nc.gpsimd.iota(node0[:], pattern=[[1, P]], base=0, channel_multiplier=0,
                                   allow_small_or_imprecise_dtypes=True).then_inc(s_const, 1)
                    nc.gpsimd.iota(block_base[:], pattern=[[P, NB + 1]], base=0, channel_multiplier=0,
                                   allow_small_or_imprecise_dtypes=True).then_inc(s_const, 1)
                    nc.gpsimd.iota(block_end[:], pattern=[[P, NB]], base=P, channel_multiplier=0,
                                   allow_small_or_imprecise_dtypes=True).then_inc(s_const, 1)
                    nc.gpsimd.memset(ones_row[:], 1.0).then_inc(s_const, 1)
                    nc.gpsimd.memset(ones_col[:], 1.0).then_inc(s_const, 1)
                    nc.gpsimd.memset(ring[:, :, :, D:D + 1], 1.0).then_inc(s_const, 1)
                    nc.gpsimd.memset(eps[:], LN_EPS).then_inc(s_const, 1)
                    pool.wait_ge(s_src, EDGE_DMAS)
                    nc.gpsimd.tensor_copy(src_f[:], src_i[:]).then_inc(s_srcf, 1)

                @block.vector
                def _(dve):
                    dve.wait_ge(s_dst, EDGE_DMAS)
                    nc.vector.tensor_copy(dst_f[:], dst_i[:]).then_inc(s_conv, 1)
                    dve.wait_ge(s_nxt, EDGE_DMAS)
                    nc.vector.tensor_copy(nxt_f[:], nxt_i[:]).then_inc(s_dve0, 1)
                    dve.wait_ge(s_dve0, 1)
                    dve.wait_ge(s_conv, 1)
                    nc.vector.tensor_tensor(nxt_f[:], dst_f[:], nxt_f[:], ALU.is_gt).then_inc(s_dve0, 1)
                    dve.wait_ge(s_dve0, 2)
                    nc.vector.reduce_sum(falls[:], nxt_f[:], AX.XY).then_inc(s_cmp, 1)
                    dve.wait_ge(s_const, 8)
                    for c in range(CH):
                        nc.vector.tensor_scalar(compared[:, c, :], block_end[0:PR, :], dst_f[:, c, 0:1], None,
                                                ALU.is_gt).then_inc(s_cmp, 1)
                    dve.wait_ge(s_count, 1)
                    nc.vector.tensor_copy(hi_raw[:], lg_hi).then_inc(s_dve0, 1)
                    dve.wait_ge(s_dve0, 3)
                    nc.vector.tensor_scalar(unsorted[:, 0:1], hi_raw[:, NB:NB + 1], 1.0, None,
                                            ALU.min).then_inc(s_dve0, 1)
                    nc.vector.tensor_scalar(hi_raw[:, 0:NB], hi_raw[:, 0:NB], 1.0, None, ALU.max).then_inc(s_dve0, 1)
                    dve.wait_ge(s_dve0, 5)
                    nc.vector.tensor_scalar(unsorted[:, 1:2], unsorted[:, 0:1], -1.0, 1.0, ALU.mult,
                                            ALU.add).then_inc(s_dve0, 1)
                    dve.wait_ge(s_dve0, 6)
                    lohi = plan_f[:, 0:2 * NB + 2].rearrange("o (b two) -> o b two", two=2)
                    nc.vector.memset(plan_f[:], 1.0).then_inc(s_dve0, 1)
                    dve.wait_ge(s_dve0, 7)
                    nc.vector.memset(lohi[:, 0, 0:1], 0.0).then_inc(s_dve0, 1)
                    nc.vector.tensor_scalar(lohi[:, 1:NB, 0], hi_raw[:, 0:NB - 1], -1.0, unsorted[:, 1:2],
                                            ALU.add, ALU.mult).then_inc(s_dve0, 1)
                    nc.vector.tensor_scalar(all_pairs[:], unsorted[:, 0:1], float(PAIRS), None,
                                            ALU.mult).then_inc(s_dve0, 1)
                    dve.wait_ge(s_dve0, 10)
                    nc.vector.tensor_scalar(lohi[:, 0:NB, 1], hi_raw[:, 0:NB], all_pairs[:], None,
                                            ALU.max).then_inc(s_dve0, 1)
                    nc.vector.tensor_scalar(plan_f[:, 2 * NB + 2:], unsorted[:], float(NB - 1), 1.0, ALU.mult,
                                            ALU.add).then_inc(s_dve0, 1)
                    dve.wait_ge(s_dve0, 12)
                    nc.vector.tensor_copy(plan[:], plan_f[:]).then_inc(s_plan, 1)
                    dst_v = dst_t[:].rearrange("p (v h) -> p v h", h=2)
                    src_v = src_t[:, 0:PAIRS * 2].rearrange("p (v h) -> p v h", h=2)
                    for i in range(2 * NTURN):
                        c, h = (i % NTURN) // 2, i % 2
                        to = (dst_v if i < NTURN else src_v)[:, c * PR:(c + 1) * PR, h]
                        dve.wait_ge(s_turned, i + 1)
                        nc.vector.tensor_copy(to, turn_ps[i % 2][:, 0:PR]).then_inc(s_moved, 1)
                    dve.wait_ge(s_moved, 2 * NTURN)
                    nc.vector.tensor_copy(src_t[:, GROUPS * SLOTS:], src_t[:, 0:SLOTS]).then_inc(s_tables, 1)
                    for g in range(XG):
                        a, b = xrange(g)
                        both = b == NB and TAIL < P and b - 1 > a
                        dve.wait_ge(s_x[g], 32 if both else 16)
                        for t in range(a, b):
                            nc.vector.bn_stats(stats[:, t, :], z_res[:, t, :]).then_inc(s_stat, 1)
                        for t in range(a, b):
                            dve.wait_ge(s_stat, t + 1)
                            nc.vector.bn_aggr(mv[:, t, :], stats[:, t, :]).then_inc(s_aggr, 1)
                        dve.wait_ge(s_std, g + 1)
                        nc.vector.reciprocal(rstd[:, a:b], std[:, a:b]).then_inc(s_norm, 1)
                        dve.wait_ge(s_norm, 2 * g + 1)
                        nc.vector.scalar_tensor_tensor(out=nbias[:, a:b], in0=mv[:, a:b, 0], scalar=-1.0,
                                                       in1=rstd[:, a:b], op0=ALU.mult,
                                                       op1=ALU.mult).then_inc(s_norm, 1)

                @block.scalar
                def _(act):
                    act.wait_ge(s_const, 8)
                    for g in range(XG):
                        a, b = xrange(g)
                        act.wait_ge(s_aggr, b)
                        nc.scalar.activation(std[:, a:b], mv[:, a:b, 1], ACT.Sqrt, bias=eps[:, 0:1]).then_inc(s_std, 1)
                        act.wait_ge(s_norm, 2 * g + 2)
                        for t in range(a, b):
                            nc.scalar.activation(z_res[:, t, :], z_res[:, t, :], ACT.Relu,
                                                 bias=nbias[:, t:t + 1], scale=rstd[:, t:t + 1]).then_inc(s_h, 1)

                @block.tensor
                def _(pe):
                    pe.wait_ge(s_const, 8)
                    pe.wait_ge(s_cmp, 1 + CH)
                    for c in range(CH):
                        pe.matmul(lg_hi[:, 0:NB], ones_col[0:PR, :], compared[:, c, :], start=(c == 0),
                                  stop=(c == CH - 1))
                    pe.matmul(lg_hi[:, NB:NB + 1], ones_col[0:PR, :], falls[:], start=True,
                              stop=True).then_inc(s_count, 1)
                    for i in range(2 * NTURN):
                        c, h = (i % NTURN) // 2, i % 2
                        if i == NTURN:
                            pe.wait_ge(s_srcf, 1)
                        rows = (dst_f if i < NTURN else src_f)[:, c, h * P:(h + 1) * P]
                        if i >= 2:
                            pe.wait_ge(s_moved, i - 1)
                        pe.transpose(turn_ps[i % 2][:, 0:PR], rows, ident[0:PR, 0:PR]).then_inc(s_turned, 1)

            def block_no(eng, p, b):
                return nc.s_assert_within(eng.snap(p + b), 0, NB - 1,
                                          skip_runtime_bounds_check_because="passes * blocks_per_pass = NB")

            def passes_of(eng):
                return (eng.value_load(plan[0:1, 2 * NB + 2:2 * NB + 3], min_val=1, max_val=NB),
                        eng.value_load(plan[0:1, 2 * NB + 3:2 * NB + 4], min_val=1, max_val=NB))

            def pairs_of(eng, blk):
                lo = eng.value_load(plan[0:1, bass.ds(blk * 2, 1)], min_val=0, max_val=PAIRS - 1)
                hi = eng.value_load(plan[0:1, bass.ds(blk * 2 + 1, 1)], min_val=1, max_val=PAIRS)
                return lo, hi

            def steps_of(eng, p, b):
                return eng.snap(p * PAIRS + b)

            def pair_no(u):
                return nc.s_assert_within(u, 0, PAIRS - 1,
                                          skip_runtime_bounds_check_because="lo <= pair < hi <= PAIRS")

            def leading_pairs(eng, lo, hi, use):
                use(lo, 0)
                with eng.If(lo + 1 < hi):
                    use(pair_no(lo + 1), 1)
                more = eng.snap((hi + lo * (TURN - 1) + (TURN - 2)) % TURN)
                with eng.If(lo + 2 < hi):
                    for i in range(TURN - 1):
                        with eng.If(more > i):
                            use(pair_no(lo + (2 + i)), 2 + i)
                return lo + 2 + more

            def other_pairs(eng, start, hi, use):
                with eng.If(start < hi):
                    with eng.Fori(start, hi, TURN) as u:
                        for i in range(TURN):
                            use(pair_no(u + i), 1 + TURN + i)

            with nc.Block() as block:

                @block.gpsimd
                def _(pool):
                    passes, _ = passes_of(pool)
                    for l in range(L):
                        if l:
                            pool.wait_ge(s_stored[l - 1], 16 * NB)
                        else:
                            for g in range(XG):
                                pool.wait_ge(s_hst[g], 16)
                        with pool.Fori(0, passes) as p:
                            with pool.Fori(0, GROUPS) as g:
                                turn = pool.snap(p * GROUPS + g)
                                for s in range(SLOTS):
                                    if s % RING == 0:
                                        pool.wait_ge(s_idx[l][s // RING], turn * 16 + 16)
                                    if s % 2 == 0:
                                        pool.wait_ge(s_free[l], turn * RING + (s // 2 + 1))
                                        pool.sem_inc(s_begun, 1)
                                    pool.indirect_dma_start(
                                        out=ring[:, s // 2, s % 2, 0:D], out_offset=None, in_=z_dram[l],
                                        in_offset=bass.IndirectOffsetOnAxis(ap=gather_idx[:, s:s + 1], axis=0),
                                    ).then_inc(s_gath[l][s], 16)

                @block.sync
                def _(sp):
                    passes, _ = passes_of(sp)
                    for l in range(L):
                        if l:
                            for h in range(2):
                                sp.wait_ge(s_idx[l - 1][h], passes * (16 * GROUPS) + 16)
                        for h in range(2):
                            a = h * RING
                            sp.dma_start(gather_idx[:, a:a + RING], src_t[:, a:a + RING]).then_inc(s_idx[l][h], 16)
                        with sp.Fori(0, passes) as p:
                            with sp.Fori(0, GROUPS) as g:
                                turn = sp.snap(p * GROUPS + g)
                                for s in range(SLOTS):
                                    sp.wait_ge(s_gath[l][s], turn * 16 + 16)
                                    if s % 2 == 1:
                                        sp.sem_inc(s_landed[l], 1)
                                    if s % RING == RING - 1:
                                        a = s + 1 - RING
                                        sp.dma_start(gather_idx[:, a:a + RING],
                                                     src_t[:, bass.ds(g * SLOTS + (SLOTS + a), RING)]).then_inc(
                                                         s_idx[l][a // RING], 16)
                    for h in range(2):
                        sp.wait_ge(s_idx[L - 1][h], passes * (16 * GROUPS) + 16)
                    sp.sem_inc(s_staged_all, 1)

                @block.vector
                def _(dve):
                    passes, blocks = passes_of(dve)
                    dve.wait_ge(s_bias, 1)
                    nc.vector.tensor_copy(bias[:], mix_ps[0][:, 0:L * K]).then_inc(s_over, 1)
                    dve.sem_inc(s_mean, 1)

                    def compare(l, u, place, free):
                        if free is not None:
                            dve.wait_ge(s_ohf[l], free)
                        nc.vector.tensor_tensor(
                            onehot[:, place, :, :], nodes[:].unsqueeze(1).to_broadcast([P, 2, P]),
                            dst_t[:, bass.ds(u * 2, 2)].unsqueeze(2).to_broadcast([P, 2, P]),
                            ALU.is_equal).then_inc(s_ohr[l], 1)

                    next_start = dve.alloc_register("next_start")
                    next_hi = dve.alloc_register("next_hi")

                    def compare_leading(l, blk, free):
                        lo, hi = pairs_of(dve, blk)
                        dve.wait_ge(s_ohf[l], free)
                        start = leading_pairs(dve, lo, hi, lambda u, place: compare(l, u, place, None))
                        dve.reg_mov(next_start, start)
                        dve.reg_mov(next_hi, hi)

                    def number_nodes(blk, turn):
                        nc.vector.tensor_scalar(nodes[:], node0[:], block_base[:, bass.ds(blk, 1)], None,
                                                ALU.add).then_inc(s_nodes, 1)
                        dve.wait_ge(s_nodes, turn)

                    for l in range(L):
                        base = l * NB
                        number_nodes(0, l * (NB + 1) + 1)
                        compare_leading(l, 0, TURN)
                        with dve.Fori(0, passes) as p:
                            with dve.Fori(0, blocks) as b:
                                blk = block_no(dve, p, b)
                                now = dve.snap(blk + (base + 1))
                                start, hi = dve.snap(next_start), dve.snap(next_hi)
                                step0 = steps_of(dve, p, b)
                                other_pairs(dve, start, hi, lambda u, place: compare(l, u, place, step0 + u + 1))
                                dve.wait_ge(s_ohf[l], step0 + hi + TURN)
                                nc.vector.tensor_scalar(cnt[:, 0:1], agg_ps[:, D:D + 1], 1.0, None,
                                                        ALU.max).then_inc(s_cmax, 1)
                                dve.wait_ge(s_cmax, now)
                                nc.vector.reciprocal(cnt[:, 1:2], cnt[:, 0:1]).then_inc(s_rcnt, 1)
                                dve.wait_ge(s_rcnt, now)
                                nc.vector.tensor_scalar(mean[:], agg_ps[:, 0:D], cnt[:, 1:2], None,
                                                        ALU.mult).then_inc(s_mean, 1)
                                dve.wait_ge(s_logit, now)
                                nc.vector.tensor_tensor(logits[:], lg_ps[:, 0:K], bias[:, l * K:(l + 1) * K],
                                                        ALU.add).then_inc(s_biased, 1)
                                dve.wait_ge(s_biased, now)
                                nc.vector.tensor_reduce(negmax[:], logits[:], AX.X, ALU.max,
                                                        negate=True).then_inc(s_nmax, 1)
                                number_nodes(blk + 1, now + (l + 1))
                                dve.wait_ge(s_ex, now)
                                nc.vector.reciprocal(rsum[:], ex[:, K:K + 1]).then_inc(s_rsum, 1)
                                dve.wait_ge(s_rsum, now)
                                nc.vector.tensor_scalar(wts[:], ex[:], rsum[:, 0:1], None, ALU.mult).then_inc(s_wts, 1)
                                compare_leading(l, blk + 1, step0 + hi + TURN)
                                dve.wait_ge(s_wts, now)
                                dve.wait_ge(s_zs, now)
                                for k in range(K):
                                    i, j = divmod(k * D, HALF)
                                    if j == 0:
                                        dve.wait_ge(s_half[i], now)
                                    if k:
                                        dve.wait_ge(s_mix[k - 1], now)
                                    nc.vector.scalar_tensor_tensor(
                                        out=mix[:], in0=mix_ps[i][:, j:j + D], scalar=wts[:, k:k + 1], in1=mix[:],
                                        op0=ALU.mult, op1=ALU.add).then_inc(s_mix[k] if k < K - 1 else s_over, 1)
                                if l == L - 1:
                                    dve.wait_ge(s_over, now + 1)
                                    nc.vector.scalar_tensor_tensor(out=z_out[:], in0=mix[:], scalar=0.0, in1=x_in[:],
                                                                   op0=ALU.max, op1=ALU.add).then_inc(s_res, 1)

                @block.scalar
                def _(act):
                    passes, blocks = passes_of(act)

                    def take_z(blk):
                        nc.scalar.activation(z_in[:], z_res[:, bass.ds(blk, 1), :], ACT.Copy).then_inc(s_zin, 1)

                    def copy_zT(count):
                        act.wait_ge(s_zturn, count)
                        nc.scalar.activation(zT[:], zT_ps[:], ACT.Copy).then_inc(s_zT, 1)

                    nc.scalar.activation(negmax[:], ones_col[:], ACT.Exp)
                    for l in range(L):
                        base = l * NB
                        last = l == L - 1
                        if l:
                            act.wait_ge(s_res, base)
                        take_z(0)
                        copy_zT(l * (NB + 1) + 1)
                        with act.Fori(0, passes) as p:
                            with act.Fori(0, blocks) as b:
                                blk = block_no(act, p, b)
                                now = act.snap(blk + (base + 1))
                                if last:
                                    with act.If(blk < NB - 1):
                                        whole = nc.s_assert_within(blk, 0, NB - 2,
                                                                   skip_runtime_bounds_check_because="just compared")
                                        act.dma_start(x_in[:], x[bass.ds(whole * P, P), :]).then_inc(s_xio, 16)
                                    with act.Else():
                                        act.dma_start(x_in[0:TAIL, :], x[(NB - 1) * P:N, :]).then_inc(s_xio, 16)
                                take_z(blk + 1)
                                act.wait_ge(s_nmax, now)
                                nc.scalar.activation(ex[:, 0:K], logits[:], ACT.Exp, bias=negmax[:, 0:1],
                                                     accum_out=ex[:, K:K + 1]).then_inc(s_ex, 1)
                                act.wait_ge(s_mturn, now)
                                nc.scalar.activation(meanT[:], mT_ps[:], ACT.Copy).then_inc(s_mT, 1)
                                if last:
                                    act.wait_ge(s_xio, blk * 32 + 16)
                                act.wait_ge(s_wts, now)
                                act.sem_inc(s_past, 1)
                                nc.scalar.activation(mix[:], z_res[:, bass.ds(blk, 1), :], ACT.Copy,
                                                     scale=wts[:, K:K + 1]).then_inc(s_zs, 1)
                                copy_zT(now + (l + 1))
                                if not last:
                                    act.wait_ge(s_over, now + 1)
                                    act.sem_inc(s_past, 1)
                                    nc.scalar.activation(z_res[:, bass.ds(blk, 1), :], mix[:],
                                                         ACT.Relu).then_inc(s_res, 1)
                                    act.wait_ge(s_res, now)
                                    act.dma_start(z_dram[l + 1][bass.ds(blk * P, P), :],
                                                  z_res[:, bass.ds(blk, 1), :]).then_inc(s_stored[l], 16)
                                else:
                                    with act.If(blk < NB - 1):
                                        whole = nc.s_assert_within(blk, 0, NB - 2,
                                                                   skip_runtime_bounds_check_because="just compared")
                                        act.wait_ge(s_res, now)
                                        act.dma_start(out[bass.ds(whole * P, P), :], z_out[:]).then_inc(s_xio, 16)
                                    with act.Else():
                                        act.wait_ge(s_res, now)
                                        act.dma_start(out[(NB - 1) * P:N, :], z_out[0:TAIL, :]).then_inc(s_xio, 16)
                    act.wait_ge(s_xio, 2 * 16 * NB)

                @block.tensor
                def _(pe):
                    passes, blocks = passes_of(pe)
                    pe.matmul(mix_ps[0][:, 0:L * K], ones_row[:], envb_sb[0:1, :, :], start=True,
                              stop=True).then_inc(s_bias, 1)
                    for l in range(L):
                        base = l * NB
                        pe.sem_inc(s_free[l], RING)
                        pe.sem_inc(s_ohf[l], TURN)

                        def add_pair(u, place, step, landed, first):
                            pe.wait_ge(s_landed[l], landed)
                            pe.wait_ge(s_ohr[l], step + 1)
                            for h in range(2):
                                mm = pe.matmul(agg_ps[:, :], onehot[:, place, h, :],
                                               ring[:, bass.ds(u % RING, 1), h, 0:D + 1],
                                               start=first and h == 0, stop=True, skip_group_check=True)
                                if h == 1:
                                    mm.then_inc(s_ohf[l], 1)
                                elif not first:
                                    mm.then_inc(s_free[l], 1)

                        def turn_z(count):
                            pe.wait_ge(s_zin, count)
                            for c in range(DC):
                                mm = pe.transpose(zT_ps[:, c, :], z_in[:, c * P:(c + 1) * P], ident[:])
                            mm.then_inc(s_zturn, 1)

                        turn_z(l * (NB + 1) + 1)
                        with pe.Fori(0, passes) as p:
                            with pe.Fori(0, blocks) as b:
                                blk = block_no(pe, p, b)
                                now = pe.snap(blk + (base + 1))
                                lo, hi = pairs_of(pe, blk)
                                step0 = steps_of(pe, p, b)
                                land0 = pe.snap(p * PAIRS + 1)
                                pe.wait_ge(s_mean, now)

                                def add(u, place):
                                    add_pair(u, place, step0 + u, land0 + u, place == 0)

                                start = pe.snap(leading_pairs(pe, lo, hi, add))
                                other_pairs(pe, start, hi, add)
                                pe.wait_ge(s_zT, now + l)
                                for c in range(DC):
                                    mm = pe.matmul(lg_ps[:, 0:K], zT[:, c, :], envw_sb[:, l, c, :], start=(c == 0),
                                                   stop=(c == DC - 1))
                                mm.then_inc(s_logit, 1)

                                def product(lhsT, c, i, **flags):
                                    w = w_sb[:, l, c, :, :].rearrange("p k o -> p (k o)")
                                    return pe.matmul(mix_ps[i][:, :], lhsT, w[:, i * HALF:(i + 1) * HALF], **flags)

                                pe.wait_ge(s_over, now)
                                for i in range(2):
                                    product(zT[:, 0, :], DC, i, start=True, stop=False)
                                pe.wait_ge(s_mean, now + 1)
                                for c in range(DC):
                                    mm = pe.transpose(mT_ps[:, c, :], mean[:, c * P:(c + 1) * P], ident[:])
                                mm.then_inc(s_mturn, 1)
                                for i in range(2):
                                    for c in range(1, DC):
                                        product(zT[:, c, :], DC + c, i, start=False, stop=False)
                                pe.wait_ge(s_mT, now)
                                for i in range(2):
                                    for c in range(DC):
                                        mm = product(meanT[:, c, :], c, i, start=False, stop=(c == DC - 1))
                                    mm.then_inc(s_half[i], 1)
                                turn_z(now + (l + 1))
                            pe.drain().then_inc(s_free[l], 1)


_INS = ["x", "src", "dst", "L0_gnn_W", "L0_gnn_envW", "L0_gnn_envb"]


def kernel(**inputs):
    import numpy as np
    import concourse.bacc as bacc
    from concourse.bass_utils import run_bass_kernel_spmd

    nc = bacc.Bacc("TRN2", target_bir_lowering=False, num_devices=1)
    arrays, args = {}, []
    for name in _INS:
        a = np.ascontiguousarray(inputs[name])
        arrays[f"in_{name}"] = a
        args.append(nc.dram_tensor(f"in_{name}", a.shape, mybir.dt.from_np(a.dtype), kind="ExternalInput").ap())
    out = nc.dram_tensor("out_x", arrays["in_x"].shape, F32, kind="ExternalOutput").ap()
    gnn_kernel(nc, *args, out)
    r = run_bass_kernel_spmd(nc, [arrays], core_ids=[0])
    return r.results[0]["out_x"]
```

```python
from contextlib import ExitStack

import concourse.bass as bass
from concourse import mybir

P = 128
ALU = mybir.AluOpType
ACT = mybir.ActivationFunctionType
AX = mybir.AxisListType
F32 = mybir.dt.float32
I32 = mybir.dt.int32
LN_EPS = 1e-5

RING = 16
ROW = 264
NO_NODE = 1 << 20
TURN = 4
PLACES = 2 + (TURN - 1) + TURN
LOAD = 7
EARLY = 24


def gnn_kernel(nc, x, src, dst, W, envW, envb, out):
    N, D = x.shape
    E = src.shape[0]
    L, K, D2, _ = W.shape
    DC = D // P
    CC = D2 // P
    NB = -(-N // P)
    TAIL = N - (NB - 1) * P
    GROUPS = -(-E // (2 * P * RING))
    PAIRS = GROUPS * RING
    CH = next(c for c in range(1, 99) if PAIRS % c == 0 and PAIRS // c <= P)
    PR = PAIRS // CH
    FULL, REST = divmod(E, 2 * P)
    XG = -(-NB // LOAD)
    SLOTS = 2 * RING
    HALF = K * D // 2
    assert PAIRS <= HALF

    ctx = ExitStack()

    def sb(name, shape, dt=F32):
        return ctx.enter_context(nc.sbuf_tensor(name, shape, dt))

    def psum(name, shape):
        return ctx.enter_context(nc.psum_tensor(name, shape, F32))

    def sem(name):
        return ctx.enter_context(nc.semaphore(name))

    with ctx:
        z_dram = [nc.dram_tensor(f"z{l}_dram", (NB * P, D), F32).ap() for l in range(L)]

        z_res = sb("z_res", [P, NB + 1, D])
        x_in = sb("x_in", [P, D])
        w_sb = sb("w_sb", [P, L, CC, K, D])
        envw_sb = sb("envw_sb", [P, L, DC, K])
        envb_sb = sb("envb_sb", [1, L, K])
        ring = sb("ring", [P, RING, 2, ROW])
        ident = sb("ident", [P, P])
        ones_row = sb("ones_row", [1, P])
        ones_col = sb("ones_col", [P, 1])
        node0 = sb("node0", [P, P])
        block_base = sb("block_base", [P, NB + 1])
        block_end = sb("block_end", [P, NB])
        src_t = sb("src_t", [P, (GROUPS + 1) * SLOTS], I32)
        dst_t = sb("dst_t", [P, PAIRS * 2])
        gather_idx = sb("gather_idx", [P, SLOTS], I32)
        plan_f = sb("plan_f", [1, 2 * NB + 4])
        plan = sb("plan", [1, 2 * NB + 4], I32)
        hi_raw = sb("hi_raw", [1, NB + 1])
        unsorted = sb("unsorted", [1, 2])
        onehot = sb("onehot", [P, PLACES, 2, P])
        z_in = sb("z_in", [P, D])
        zT = sb("zT", [P, DC, P])
        mean = sb("mean", [P, D])
        meanT = sb("meanT", [P, DC, P])
        cnt = sb("cnt", [P, 2])
        bias = sb("bias", [P, L * K])
        logits = sb("logits", [P, K])
        negmax = sb("negmax", [P, 1])
        ex = sb("ex", [P, K + 1])
        rsum = sb("rsum", [P, 1])
        wts = sb("wts", [P, K + 1])
        mix = sb("mix", [P, D])
        z_out = sb("z_out", [P, D])

        agg_ps = psum("agg_ps", [P, D + 1])
        zT_ps = psum("zT_ps", [P, DC, P])
        mT_ps = psum("mT_ps", [P, DC, P])
        lg_ps = psum("lg_ps", [P, max(K, NB + 1)])
        nodes = psum("nodes", [P, P])
        mix_ps = [psum(f"mix{i}_ps", [P, HALF]) for i in range(2)]
        lg_hi = lg_ps[0:1, 0:NB + 1]

        s_src = sem("src_loaded")
        s_dst = sem("dst_loaded")
        s_nxt = sem("next_dst_loaded")
        s_env = sem("env_weights_loaded")
        s_w = [sem(f"weights{l}_loaded") for l in range(L)]
        s_x = [sem(f"x{g}_loaded") for g in range(XG)]
        s_pad = sem("pads_written")
        s_const = sem("constants_ready")
        s_dve0 = sem("vector_prep_step")
        s_pool0 = sem("gpsimd_prep_step")
        s_dstf = sem("dst_as_float")
        s_fall = sem("falls_found")
        s_srcf = sem("src_as_float")
        s_turned = sem("edges_turned")
        s_moved = sem("turned_edges_moved")
        s_cmp = sem("pair_compared")
        s_count = sem("plan_counted")
        s_plan = sem("plan_ready")
        s_tables = sem("edge_tables_ready")
        s_stat = sem("x_stats_ready")
        s_aggr = sem("x_mean_var_ready")
        s_std = sem("x_std_ready")
        s_norm = sem("norm_terms_ready")
        s_h = sem("h_computed")
        s_gath = [[sem(f"gathered{l}_{s}") for s in range(SLOTS)] for l in range(L)]
        s_idx = [[sem(f"idx_staged{l}_{h}") for h in range(2)] for l in range(L)]
        s_landed = [sem(f"pairs_landed{l}") for l in range(L)]
        s_free = [sem(f"pairs_free{l}") for l in range(L)]
        s_ohr = [sem(f"onehots_ready{l}") for l in range(L)]
        s_ohf = [sem(f"onehots_free{l}") for l in range(L)]
        s_past = sem("act_past_wait")
        s_begun = sem("pairs_begun")
        s_staged_all = sem("staging_over")
        s_nodes = sem("nodes_ready")
        s_zin = sem("z_loaded")
        s_cmax = sem("count_clamped")
        s_rcnt = sem("count_inverted")
        s_mean = sem("mean_ready")
        s_zturn = sem("z_turned")
        s_zT = sem("zT_ready")
        s_mturn = sem("mean_turned")
        s_mT = sem("meanT_ready")
        s_bias = sem("biases_spread")
        s_biasm = sem("biases_moved")
        s_logit = sem("logits_ready")
        s_biased = sem("logits_biased")
        s_nmax = sem("negmax_ready")
        s_ex = sem("exp_ready")
        s_rsum = sem("sum_inverted")
        s_wts = sem("weights_ready")
        s_zs = sem("z_scaled")
        s_half = [sem(f"mix_half{i}_ready") for i in range(2)]
        s_mix = [sem(f"mix_step{k}") for k in range(K - 1)]
        s_over = sem("block_over")
        s_res = sem("result_ready")
        s_stored = [sem(f"z{l + 1}_stored") for l in range(L - 1)]
        s_xio = sem("x_loaded_or_out_stored")
        s_hst = [sem(f"h{g}_stored") for g in range(XG)]

        edge_ctx = ExitStack()

        def ed(name, shape, dt=F32):
            return edge_ctx.enter_context(nc.sbuf_tensor(name, shape, dt))

        with edge_ctx:
            src_i = ed("src_i", [PR, CH, 2 * P], I32)
            dst_i = ed("dst_i", [PR, CH, 2 * P], I32)
            nxt_i = ed("nxt_i", [PR, CH, 2 * P], I32)
            src_f = ed("src_f", [PR, CH, 2 * P])
            dst_f = ed("dst_f", [PR, CH, 2 * P])
            fall = ed("fall", [PR, CH, 2 * P])
            compared = ed("compared", [PR, CH, NB])
            falls = ed("falls", [PR, 1])
            stats = ed("stats", [P, NB + EARLY, 6])
            mv = ed("mv", [P, NB + EARLY, 2])
            std = ed("std", [P, NB + EARLY])
            all_pairs = ed("all_pairs", [1, 1])
            rstd = ed("rstd", [P, NB + EARLY])
            nbias = ed("nbias", [P, NB + EARLY])
            eps = ed("eps", [P, 1])
            warm = ed("warm", [1, 1])

            def load_edges(eng, tile_i, array, first, signal):
                n = E - first
                full, rest = divmod(n, 2 * P)
                whole = min(full // PR, CH)
                eng.dma_start(tile_i[:, 0:whole, :], array[first:first + whole * PR * 2 * P].rearrange(
                    "(c p e) -> p c e", p=PR, e=2 * P)).then_inc(signal, 16)
                left = full - whole * PR
                if left:
                    a = first + whole * PR * 2 * P
                    eng.dma_start(tile_i[0:left, whole, :], array[a:a + left * 2 * P].rearrange(
                        "(p e) -> p e", e=2 * P)).then_inc(signal, 16)
                a = first + full * 2 * P
                eng.dma_start(tile_i[left:left + 1, whole, 0:rest], array[a:a + rest].rearrange(
                    "(o e) -> o e", o=1)).then_inc(signal, 16)
                return 16 * (3 if left else 2)

            WHOLE = FULL // PR
            EDGE_DMAS = 16 * (3 if FULL - WHOLE * PR else 2)

            def xrange(g):
                return g * LOAD, min((g + 1) * LOAD, NB)

            groups = [xrange(g) for g in range(XG)] + [(NB + s, NB + min(s + 8, EARLY)) for s in range(0, EARLY, 8)]

            def gather_first(pool, s, table):
                pool.indirect_dma_start(
                    out=ring[:, s // 2, s % 2, 0:D], out_offset=None, in_=table,
                    in_offset=bass.IndirectOffsetOnAxis(ap=src_t[:, s:s + 1], axis=0),
                ).then_inc(s_gath[0][s], 16)

            def load_weights(eng, l):
                for c in range(CC):
                    eng.dma_start(w_sb[:, l, c, :, :], W[l, :, c * P:(c + 1) * P, :].rearrange(
                        "k p o -> p k o")).then_inc(s_w[l], 16)

            def rows(t):
                return z_res[:, t, :] if t < NB else ring[:, (t - NB) // 2, (t - NB) % 2, 0:D]

            with nc.Block() as block:

                @block.sync
                def _(sp):
                    def load_x(g):
                        a, b = xrange(g)
                        full = b - 1 if b == NB and TAIL < P else b
                        if b == NB and TAIL < P:
                            sp.wait_ge(s_pad, 4)
                            sp.dma_start(z_res[0:TAIL, NB - 1, :], x[(NB - 1) * P:N, :]).then_inc(s_x[g], 16)
                        if full > a:
                            sp.dma_start(z_res[:, a:full, :], x[a * P:full * P, :].rearrange(
                                "(t p) d -> p t d", p=P)).then_inc(s_x[g], 16)

                    sp.wait_ge(s_pad, 1)
                    load_edges(sp, src_i, src, 0, s_src)
                    load_x(0)
                    sp.wait_ge(s_pad, 3)
                    load_edges(sp, dst_i, dst, 0, s_dst)
                    for g in range(1, XG - 1):
                        load_x(g)
                    load_edges(sp, nxt_i, dst, 1, s_nxt)
                    for g in range(max(XG - 1, 1), XG):
                        load_x(g)
                    sp.dma_start(envb_sb[0:1, :, :], envb.rearrange("(o l) k -> o l k", o=1)).then_inc(s_env, 16)
                    for l in range(L):
                        with nc.allow_non_contiguous_dma(reason="16-byte rows, once"):
                            sp.dma_start(envw_sb[:, l, :, :], envW[l].rearrange(
                                "(c p) k -> p c k", p=P)).then_inc(s_env, 16)
                    for g in range(XG):
                        a, b = xrange(g)
                        sp.wait_ge(s_h, b)
                        sp.dma_start(z_dram[0][a * P:b * P, :].rearrange("(t p) d -> p t d", p=P),
                                     z_res[:, a:b, :]).then_inc(s_hst[g], 16)
                    load_weights(sp, 0)

                @block.gpsimd
                def _(pool):
                    last = CH - 1
                    nc.gpsimd.memset(src_i[:, last, :], 0).then_inc(s_pad, 1)
                    nc.gpsimd.memset(dst_i[:, last, :], NO_NODE).then_inc(s_pad, 1)
                    nc.gpsimd.memset(nxt_i[:, last, :], NO_NODE).then_inc(s_pad, 1)
                    nc.gpsimd.memset(z_res[:, NB - 1:NB + 1, :], 0.0).then_inc(s_pad, 1)
                    nc.gpsimd.memset(ident[:], 0.0).then_inc(s_pool0, 1)
                    pool.wait_ge(s_pool0, 1)
                    nc.gpsimd.affine_select(out=ident[:], in_=ident[:], compare_op=ALU.not_equal, fill=1.0, base=0,
                                            pattern=[[-1, P]], channel_multiplier=1).then_inc(s_const, 1)
                    nc.gpsimd.iota(node0[:], pattern=[[1, P]], base=0, channel_multiplier=0,
                                   allow_small_or_imprecise_dtypes=True).then_inc(s_const, 1)
                    nc.gpsimd.iota(block_base[:], pattern=[[P, NB + 1]], base=0, channel_multiplier=0,
                                   allow_small_or_imprecise_dtypes=True).then_inc(s_const, 1)
                    nc.gpsimd.iota(block_end[:], pattern=[[P, NB]], base=P, channel_multiplier=0,
                                   allow_small_or_imprecise_dtypes=True).then_inc(s_const, 1)
                    nc.gpsimd.memset(ones_row[:], 1.0).then_inc(s_const, 1)
                    nc.gpsimd.memset(ones_col[:], 1.0).then_inc(s_const, 1)
                    nc.gpsimd.memset(ring[:, :, :, D:D + 1], 1.0).then_inc(s_const, 1)
                    nc.gpsimd.memset(eps[:], LN_EPS).then_inc(s_const, 1)
                    pool.wait_ge(s_moved, 2)
                    for s in range(EARLY):
                        gather_first(pool, s, x)

                @block.vector
                def _(dve):
                    def row_stats(g):
                        a, b = groups[g]
                        if g < XG:
                            both = b == NB and TAIL < P and b - 1 > a
                            dve.wait_ge(s_x[g], 32 if both else 16)
                        for t in range(a, b):
                            if g >= XG:
                                dve.wait_ge(s_gath[0][t - NB], 16)
                            nc.vector.bn_stats(stats[:, t, :], rows(t)).then_inc(s_stat, 1)
                        for t in range(a, b):
                            dve.wait_ge(s_stat, t + 1)
                            nc.vector.bn_aggr(mv[:, t, :], stats[:, t, :]).then_inc(s_aggr, 1)

                    def row_norms(g):
                        a, b = groups[g]
                        dve.wait_ge(s_std, g + 1)
                        nc.vector.reciprocal(rstd[:, a:b], std[:, a:b]).then_inc(s_norm, 1)
                        dve.wait_ge(s_norm, 2 * g + 1)
                        nc.vector.scalar_tensor_tensor(out=nbias[:, a:b], in0=mv[:, a:b, 0], scalar=-1.0,
                                                       in1=rstd[:, a:b], op0=ALU.mult,
                                                       op1=ALU.mult).then_inc(s_norm, 1)

                    def convert(to, tile_i, loaded, done):
                        dve.wait_ge(loaded, EDGE_DMAS)
                        nc.vector.tensor_copy(to[:], tile_i[:]).then_inc(done, 1)

                    def compare_pairs():
                        convert(dst_f, dst_i, s_dst, s_dstf)
                        dve.wait_ge(s_dstf, 1)
                        dve.wait_ge(s_const, 8)
                        for c in range(CH):
                            nc.vector.tensor_scalar(compared[:, c, :], block_end[0:PR, :], dst_f[:, c, 0:1], None,
                                                    ALU.is_gt).then_inc(s_cmp, 1)

                    def move_turned(i):
                        table, h = (src_t, dst_t)[i // 2], i % 2
                        dve.wait_ge(s_turned, i + 1)
                        nc.vector.tensor_copy(table[:, 0:PAIRS * 2].rearrange("p (v h) -> p v h", h=2)[:, :, h],
                                              mix_ps[h][:, 0:PAIRS]).then_inc(s_moved, 1)

                    def sum_falls():
                        dve.wait_ge(s_nxt, EDGE_DMAS)
                        nc.vector.tensor_tensor(fall[:], dst_i[:], nxt_i[:], ALU.is_gt).then_inc(s_fall, 1)
                        dve.wait_ge(s_fall, 1)
                        nc.vector.reduce_sum(falls[:], fall[:], AX.XY).then_inc(s_cmp, 1)

                    def end_tables():
                        dve.wait_ge(s_moved, 2)
                        nc.vector.tensor_copy(src_t[:, GROUPS * SLOTS:], src_t[:, 0:SLOTS]).then_inc(s_tables, 1)

                    def make_plan():
                        dve.wait_ge(s_count, 1)
                        nc.vector.tensor_copy(hi_raw[:], lg_hi).then_inc(s_dve0, 1)
                        dve.wait_ge(s_dve0, 1)
                        nc.vector.tensor_scalar(unsorted[:, 0:1], hi_raw[:, NB:NB + 1], 1.0, None,
                                                ALU.min).then_inc(s_dve0, 1)
                        nc.vector.tensor_scalar(hi_raw[:, 0:NB], hi_raw[:, 0:NB], 1.0, None, ALU.max).then_inc(s_dve0, 1)
                        dve.wait_ge(s_dve0, 3)
                        nc.vector.tensor_scalar(unsorted[:, 1:2], unsorted[:, 0:1], -1.0, 1.0, ALU.mult,
                                                ALU.add).then_inc(s_dve0, 1)
                        dve.wait_ge(s_dve0, 4)
                        lohi = plan_f[:, 0:2 * NB + 2].rearrange("o (b two) -> o b two", two=2)
                        nc.vector.memset(plan_f[:], 1.0).then_inc(s_dve0, 1)
                        dve.wait_ge(s_dve0, 5)
                        nc.vector.memset(lohi[:, 0, 0:1], 0.0).then_inc(s_dve0, 1)
                        nc.vector.tensor_scalar(lohi[:, 1:NB, 0], hi_raw[:, 0:NB - 1], -1.0, unsorted[:, 1:2],
                                                ALU.add, ALU.mult).then_inc(s_dve0, 1)
                        nc.vector.tensor_scalar(all_pairs[:], unsorted[:, 0:1], float(PAIRS), None,
                                                ALU.mult).then_inc(s_dve0, 1)
                        dve.wait_ge(s_dve0, 8)
                        nc.vector.tensor_scalar(lohi[:, 0:NB, 1], hi_raw[:, 0:NB], all_pairs[:], None,
                                                ALU.max).then_inc(s_dve0, 1)
                        nc.vector.tensor_scalar(plan_f[:, 2 * NB + 2:], unsorted[:], float(NB - 1), 1.0, ALU.mult,
                                                ALU.add).then_inc(s_dve0, 1)
                        dve.wait_ge(s_dve0, 10)
                        nc.vector.tensor_copy(plan[:], plan_f[:]).then_inc(s_plan, 1)

                    convert(src_f, src_i, s_src, s_srcf)
                    move_turned(0)
                    move_turned(1)
                    pieces = [lambda: move_turned(2), lambda: move_turned(3), end_tables, sum_falls, make_plan]
                    due = [max(XG - 3 + i, 1) for i in range(len(pieces))]
                    for g in range(len(groups)):
                        row_stats(g)
                        for piece, when in zip(pieces, due):
                            if when == g:
                                piece()
                        row_norms(g)
                        if g == 0:
                            compare_pairs()
                    dve.wait_ge(s_bias, 1)
                    nc.vector.tensor_copy(bias[:], mix_ps[0][:, 0:L * K]).then_inc(s_biasm, 1)

                @block.scalar
                def _(act):
                    act.wait_ge(s_const, 8)

                    def roots(g):
                        a, b = groups[g]
                        act.wait_ge(s_aggr, b)
                        nc.scalar.activation(std[:, a:b], mv[:, a:b, 1], ACT.Sqrt, bias=eps[:, 0:1]).then_inc(s_std, 1)

                    nc.scalar.activation(warm[:], eps[0:1, :], ACT.Sqrt)
                    roots(0)
                    for g, (a, b) in enumerate(groups):
                        act.wait_ge(s_norm, 2 * g + 2)
                        for t in range(a, b):
                            if t == b - 1 and g + 1 < len(groups):
                                roots(g + 1)
                            nc.scalar.activation(rows(t), rows(t), ACT.Relu,
                                                 bias=nbias[:, t:t + 1], scale=rstd[:, t:t + 1]).then_inc(s_h, 1)

                @block.tensor
                def _(pe):
                    pe.wait_ge(s_const, 8)
                    for i in range(4):
                        edges, h = (src_f, dst_f)[i // 2], i % 2
                        pe.wait_ge((s_srcf, s_dstf)[i // 2], 1)
                        if i >= 2:
                            pe.wait_ge(s_moved, i - 1)
                        for c in range(CH):
                            mm = pe.transpose(mix_ps[h][:, c * PR:(c + 1) * PR], edges[:, c, h * P:(h + 1) * P],
                                              ident[0:PR, 0:PR])
                        mm.then_inc(s_turned, 1)
                    pe.wait_ge(s_cmp, CH + 1)
                    for c in range(CH):
                        pe.matmul(lg_hi[:, 0:NB], ones_col[0:PR, :], compared[:, c, :], start=(c == 0),
                                  stop=(c == CH - 1))
                    pe.matmul(lg_hi[:, NB:NB + 1], ones_col[0:PR, :], falls[:], start=True,
                              stop=True).then_inc(s_count, 1)
                    pe.wait_ge(s_moved, 4)
                    pe.wait_ge(s_env, 16 * (L + 1))
                    pe.matmul(mix_ps[0][:, 0:L * K], ones_row[:], envb_sb[0:1, :, :], start=True,
                              stop=True).then_inc(s_bias, 1)

            def block_no(eng, p, b):
                return nc.s_assert_within(eng.snap(p + b), 0, NB - 1,
                                          skip_runtime_bounds_check_because="passes * blocks_per_pass = NB")

            def passes_of(eng):
                return (eng.value_load(plan[0:1, 2 * NB + 2:2 * NB + 3], min_val=1, max_val=NB),
                        eng.value_load(plan[0:1, 2 * NB + 3:2 * NB + 4], min_val=1, max_val=NB))

            def pairs_of(eng, blk):
                lo = eng.value_load(plan[0:1, bass.ds(blk * 2, 1)], min_val=0, max_val=PAIRS - 1)
                hi = eng.value_load(plan[0:1, bass.ds(blk * 2 + 1, 1)], min_val=1, max_val=PAIRS)
                return lo, hi

            def steps_of(eng, p, b):
                return eng.snap(p * PAIRS + b)

            def pair_no(u):
                return nc.s_assert_within(u, 0, PAIRS - 1,
                                          skip_runtime_bounds_check_because="lo <= pair < hi <= PAIRS")

            def leading_pairs(eng, lo, hi, use):
                use(lo, 0)
                with eng.If(lo + 1 < hi):
                    use(pair_no(lo + 1), 1)
                more = eng.snap((hi + lo * (TURN - 1) + (TURN - 2)) % TURN)
                with eng.If(lo + 2 < hi):
                    for i in range(TURN - 1):
                        with eng.If(more > i):
                            use(pair_no(lo + (2 + i)), 2 + i)
                return lo + 2 + more

            def other_pairs(eng, start, hi, use):
                with eng.If(start < hi):
                    with eng.Fori(start, hi, TURN) as u:
                        for i in range(TURN):
                            use(pair_no(u + i), 1 + TURN + i)

            with nc.Block() as block:

                @block.gpsimd
                def _(pool):
                    passes, _ = passes_of(pool)
                    for l in range(L):
                        if l:
                            pool.wait_ge(s_stored[l - 1], 16 * NB)
                        else:
                            for g in range(XG):
                                pool.wait_ge(s_hst[g], 16)
                            for s in range(EARLY, SLOTS):
                                gather_first(pool, s, z_dram[0])
                        with pool.Fori(0 if l else 1, pool.snap(passes * GROUPS)) as turn:
                            for s in range(SLOTS):
                                if s % RING == 0:
                                    pool.wait_ge(s_idx[l][s // RING], turn * 16 + (16 if l else 0))
                                if s % 2 == 0:
                                    pool.wait_ge(s_free[l], turn * RING + (s // 2 + 1))
                                    pool.sem_inc(s_begun, 1)
                                pool.indirect_dma_start(
                                    out=ring[:, s // 2, s % 2, 0:D], out_offset=None, in_=z_dram[l],
                                    in_offset=bass.IndirectOffsetOnAxis(ap=gather_idx[:, s:s + 1], axis=0),
                                ).then_inc(s_gath[l][s], 16)

                @block.sync
                def _(sp):
                    passes, _ = passes_of(sp)
                    for l in range(L):
                        if l:
                            for h in range(2):
                                sp.wait_ge(s_idx[l - 1][h], passes * (16 * GROUPS) + (0 if l == 1 else 16))
                            for h in range(2):
                                a = h * RING
                                sp.dma_start(gather_idx[:, a:a + RING],
                                             src_t[:, a:a + RING]).then_inc(s_idx[l][h], 16)
                            load_weights(sp, l)
                        with sp.Fori(0, passes) as p:
                            with sp.Fori(0, GROUPS) as g:
                                turn = sp.snap(p * GROUPS + g)
                                for s in range(SLOTS):
                                    sp.wait_ge(s_gath[l][s], turn * 16 + 16)
                                    if s % 2 == 1:
                                        sp.sem_inc(s_landed[l], 1)
                                    if s % RING == RING - 1:
                                        a = s + 1 - RING
                                        sp.dma_start(gather_idx[:, a:a + RING],
                                                     src_t[:, bass.ds(g * SLOTS + (SLOTS + a), RING)]).then_inc(
                                                         s_idx[l][a // RING], 16)
                    for h in range(2):
                        sp.wait_ge(s_idx[L - 1][h], passes * (16 * GROUPS) + (16 if L > 1 else 0))
                    sp.sem_inc(s_staged_all, 1)

                @block.vector
                def _(dve):
                    passes, blocks = passes_of(dve)
                    dve.sem_inc(s_over, 1)
                    dve.sem_inc(s_mean, 1)

                    def compare(l, u, place, free):
                        if free is not None:
                            dve.wait_ge(s_ohf[l], free)
                        nc.vector.tensor_tensor(
                            onehot[:, place, :, :], nodes[:].unsqueeze(1).to_broadcast([P, 2, P]),
                            dst_t[:, bass.ds(u * 2, 2)].unsqueeze(2).to_broadcast([P, 2, P]),
                            ALU.is_equal).then_inc(s_ohr[l], 1)

                    next_start = dve.alloc_register("next_start")
                    next_hi = dve.alloc_register("next_hi")

                    def compare_leading(l, blk, free):
                        lo, hi = pairs_of(dve, blk)
                        dve.wait_ge(s_ohf[l], free)
                        start = leading_pairs(dve, lo, hi, lambda u, place: compare(l, u, place, None))
                        dve.reg_mov(next_start, start)
                        dve.reg_mov(next_hi, hi)

                    def number_nodes(blk, turn):
                        nc.vector.tensor_scalar(nodes[:], node0[:], block_base[:, bass.ds(blk, 1)], None,
                                                ALU.add).then_inc(s_nodes, 1)
                        dve.wait_ge(s_nodes, turn)

                    for l in range(L):
                        base = l * NB
                        number_nodes(0, l * (NB + 1) + 1)
                        compare_leading(l, 0, TURN)
                        with dve.Fori(0, passes) as p:
                            with dve.Fori(0, blocks) as b:
                                blk = block_no(dve, p, b)
                                now = dve.snap(blk + (base + 1))
                                start, hi = dve.snap(next_start), dve.snap(next_hi)
                                step0 = steps_of(dve, p, b)
                                other_pairs(dve, start, hi, lambda u, place: compare(l, u, place, step0 + u + 1))
                                dve.wait_ge(s_ohf[l], step0 + hi + TURN)
                                nc.vector.tensor_scalar(cnt[:, 0:1], agg_ps[:, D:D + 1], 1.0, None,
                                                        ALU.max).then_inc(s_cmax, 1)
                                dve.wait_ge(s_cmax, now)
                                nc.vector.reciprocal(cnt[:, 1:2], cnt[:, 0:1]).then_inc(s_rcnt, 1)
                                dve.wait_ge(s_rcnt, now)
                                nc.vector.tensor_scalar(mean[:], agg_ps[:, 0:D], cnt[:, 1:2], None,
                                                        ALU.mult).then_inc(s_mean, 1)
                                dve.wait_ge(s_logit, now)
                                nc.vector.tensor_tensor(logits[:], lg_ps[:, 0:K], bias[:, l * K:(l + 1) * K],
                                                        ALU.add).then_inc(s_biased, 1)
                                dve.wait_ge(s_biased, now)
                                nc.vector.tensor_reduce(negmax[:], logits[:], AX.X, ALU.max,
                                                        negate=True).then_inc(s_nmax, 1)
                                number_nodes(blk + 1, now + (l + 1))
                                dve.wait_ge(s_ex, now)
                                nc.vector.reciprocal(rsum[:], ex[:, K:K + 1]).then_inc(s_rsum, 1)
                                dve.wait_ge(s_rsum, now)
                                nc.vector.tensor_scalar(wts[:], ex[:], rsum[:, 0:1], None, ALU.mult).then_inc(s_wts, 1)
                                compare_leading(l, blk + 1, step0 + hi + TURN)
                                dve.wait_ge(s_wts, now)
                                dve.wait_ge(s_zs, now)
                                for k in range(K):
                                    i, j = divmod(k * D, HALF)
                                    if j == 0:
                                        dve.wait_ge(s_half[i], now)
                                    if k:
                                        dve.wait_ge(s_mix[k - 1], now)
                                    nc.vector.scalar_tensor_tensor(
                                        out=mix[:], in0=mix_ps[i][:, j:j + D], scalar=wts[:, k:k + 1], in1=mix[:],
                                        op0=ALU.mult, op1=ALU.add).then_inc(s_mix[k] if k < K - 1 else s_over, 1)
                                if l == L - 1:
                                    dve.wait_ge(s_over, now + 1)
                                    nc.vector.scalar_tensor_tensor(out=z_out[:], in0=mix[:], scalar=0.0, in1=x_in[:],
                                                                   op0=ALU.max, op1=ALU.add).then_inc(s_res, 1)

                @block.scalar
                def _(act):
                    passes, blocks = passes_of(act)

                    def take_z(blk):
                        nc.scalar.activation(z_in[:], z_res[:, bass.ds(blk, 1), :], ACT.Copy).then_inc(s_zin, 1)

                    def copy_zT(count):
                        act.wait_ge(s_zturn, count)
                        nc.scalar.activation(zT[:], zT_ps[:], ACT.Copy).then_inc(s_zT, 1)

                    nc.scalar.activation(negmax[:], ones_col[:], ACT.Exp)
                    for l in range(L):
                        base = l * NB
                        last = l == L - 1
                        if l:
                            act.wait_ge(s_res, base)
                        take_z(0)
                        copy_zT(l * (NB + 1) + 1)
                        with act.Fori(0, passes) as p:
                            with act.Fori(0, blocks) as b:
                                blk = block_no(act, p, b)
                                now = act.snap(blk + (base + 1))
                                if last:
                                    with act.If(blk < NB - 1):
                                        whole = nc.s_assert_within(blk, 0, NB - 2,
                                                                   skip_runtime_bounds_check_because="just compared")
                                        act.dma_start(x_in[:], x[bass.ds(whole * P, P), :]).then_inc(s_xio, 16)
                                    with act.Else():
                                        act.dma_start(x_in[0:TAIL, :], x[(NB - 1) * P:N, :]).then_inc(s_xio, 16)
                                take_z(blk + 1)
                                act.wait_ge(s_nmax, now)
                                nc.scalar.activation(ex[:, 0:K], logits[:], ACT.Exp, bias=negmax[:, 0:1],
                                                     accum_out=ex[:, K:K + 1]).then_inc(s_ex, 1)
                                act.wait_ge(s_mturn, now)
                                nc.scalar.activation(meanT[:], mT_ps[:], ACT.Copy).then_inc(s_mT, 1)
                                if last:
                                    act.wait_ge(s_xio, blk * 32 + 16)
                                act.wait_ge(s_wts, now)
                                act.sem_inc(s_past, 1)
                                nc.scalar.activation(mix[:], z_res[:, bass.ds(blk, 1), :], ACT.Copy,
                                                     scale=wts[:, K:K + 1]).then_inc(s_zs, 1)
                                copy_zT(now + (l + 1))
                                if not last:
                                    act.wait_ge(s_over, now + 1)
                                    act.sem_inc(s_past, 1)
                                    nc.scalar.activation(z_res[:, bass.ds(blk, 1), :], mix[:],
                                                         ACT.Relu).then_inc(s_res, 1)
                                    act.wait_ge(s_res, now)
                                    act.dma_start(z_dram[l + 1][bass.ds(blk * P, P), :],
                                                  z_res[:, bass.ds(blk, 1), :]).then_inc(s_stored[l], 16)
                                else:
                                    with act.If(blk < NB - 1):
                                        whole = nc.s_assert_within(blk, 0, NB - 2,
                                                                   skip_runtime_bounds_check_because="just compared")
                                        act.wait_ge(s_res, now)
                                        act.dma_start(out[bass.ds(whole * P, P), :], z_out[:]).then_inc(s_xio, 16)
                                    with act.Else():
                                        act.wait_ge(s_res, now)
                                        act.dma_start(out[(NB - 1) * P:N, :], z_out[0:TAIL, :]).then_inc(s_xio, 16)
                    act.wait_ge(s_xio, 2 * 16 * NB)

                @block.tensor
                def _(pe):
                    passes, blocks = passes_of(pe)
                    for l in range(L):
                        base = l * NB
                        pe.sem_inc(s_free[l], RING)
                        pe.sem_inc(s_ohf[l], TURN)

                        def add_pair(u, place, step, landed, first):
                            pe.wait_ge(s_landed[l], landed)
                            pe.wait_ge(s_ohr[l], step + 1)
                            for h in range(2):
                                mm = pe.matmul(agg_ps[:, :], onehot[:, place, h, :],
                                               ring[:, bass.ds(u % RING, 1), h, 0:D + 1],
                                               start=first and h == 0, stop=True, skip_group_check=True)
                                if h == 1:
                                    mm.then_inc(s_ohf[l], 1)
                                elif not first:
                                    mm.then_inc(s_free[l], 1)

                        def turn_z(count):
                            pe.wait_ge(s_zin, count)
                            for c in range(DC):
                                mm = pe.transpose(zT_ps[:, c, :], z_in[:, c * P:(c + 1) * P], ident[:])
                            mm.then_inc(s_zturn, 1)

                        turn_z(l * (NB + 1) + 1)
                        with pe.Fori(0, passes) as p:
                            with pe.Fori(0, blocks) as b:
                                blk = block_no(pe, p, b)
                                now = pe.snap(blk + (base + 1))
                                lo, hi = pairs_of(pe, blk)
                                step0 = steps_of(pe, p, b)
                                land0 = pe.snap(p * PAIRS + 1)
                                pe.wait_ge(s_mean, now)

                                def add(u, place):
                                    add_pair(u, place, step0 + u, land0 + u, place == 0)

                                start = pe.snap(leading_pairs(pe, lo, hi, add))
                                other_pairs(pe, start, hi, add)
                                pe.wait_ge(s_zT, now + l)
                                for c in range(DC):
                                    mm = pe.matmul(lg_ps[:, 0:K], zT[:, c, :], envw_sb[:, l, c, :], start=(c == 0),
                                                   stop=(c == DC - 1))
                                mm.then_inc(s_logit, 1)

                                def product(lhsT, c, i, **flags):
                                    w = w_sb[:, l, c, :, :].rearrange("p k o -> p (k o)")
                                    return pe.matmul(mix_ps[i][:, :], lhsT, w[:, i * HALF:(i + 1) * HALF], **flags)

                                pe.wait_ge(s_over, now)
                                pe.wait_ge(s_w[l], 16 * CC)
                                for i in range(2):
                                    product(zT[:, 0, :], DC, i, start=True, stop=False)
                                pe.wait_ge(s_mean, now + 1)
                                for c in range(DC):
                                    mm = pe.transpose(mT_ps[:, c, :], mean[:, c * P:(c + 1) * P], ident[:])
                                mm.then_inc(s_mturn, 1)
                                for i in range(2):
                                    for c in range(1, DC):
                                        product(zT[:, c, :], DC + c, i, start=False, stop=False)
                                pe.wait_ge(s_mT, now)
                                for i in range(2):
                                    for c in range(DC):
                                        mm = product(meanT[:, c, :], c, i, start=False, stop=(c == DC - 1))
                                    mm.then_inc(s_half[i], 1)
                                turn_z(now + (l + 1))
                            pe.drain().then_inc(s_free[l], 1)


_INS = ["x", "src", "dst", "L0_gnn_W", "L0_gnn_envW", "L0_gnn_envb"]


def kernel(**inputs):
    import numpy as np
    import concourse.bacc as bacc
    from concourse.bass_utils import run_bass_kernel_spmd

    nc = bacc.Bacc("TRN2", target_bir_lowering=False, num_devices=1)
    arrays, args = {}, []
    for name in _INS:
        a = np.ascontiguousarray(inputs[name])
        arrays[f"in_{name}"] = a
        args.append(nc.dram_tensor(f"in_{name}", a.shape, mybir.dt.from_np(a.dtype), kind="ExternalInput").ap())
    out = nc.dram_tensor("out_x", arrays["in_x"].shape, F32, kind="ExternalOutput").ap()
    gnn_kernel(nc, *args, out)
    r = run_bass_kernel_spmd(nc, [arrays], core_ids=[0])
    return r.results[0]["out_x"]
```
